# Optimizing a Trainium2 kernel written in Bass

```python
import numpy as np
import jax
import jax.numpy as jnp

def _softmax(x, axis=-1):
    return jax.nn.softmax(x, axis=axis)

def _gelu(x):
    return jax.nn.gelu(x, approximate=True)

def _silu(x):
    return jax.nn.silu(x)

def _sigmoid(x):
    return jax.nn.sigmoid(x)

def _layernorm(x, axis=-1, eps=1e-05):
    m = jnp.mean(x, axis=axis, keepdims=True)
    v = jnp.var(x, axis=axis, keepdims=True)
    return (x - m) / jnp.sqrt(v + eps)

def _scatter_add(tgt, idx, src, axis=0):
    return tgt.at[idx].add(src)

def _segment_sum(src, seg, n):
    return jax.ops.segment_sum(src, seg, n)
kernel_name = 'mk_gnn_resnorm_d2_gnn_r8_616a2f'

def setup_inputs(seed: int=0):
    np.random.seed(seed)
    _w = jnp.asarray

    def _rec_inputs():
        import jax
        import jax.numpy as jnp
        _gk = jax.random.key(seed)
        x = 8.953e-05 + 1 * jax.random.normal(jax.random.fold_in(_gk, 1), (12500, 16), jnp.float32)
        src = jax.random.randint(jax.random.fold_in(_gk, 2), (400000,), 0, 12500, jnp.int32)
        dst = jax.random.randint(jax.random.fold_in(_gk, 3), (400000,), 0, 12500, jnp.int32)
        _o = jnp.argsort(dst, stable=True)
        src = src[_o]
        dst = dst[_o]
        edge_attr_3 = -1.09012e-05 + 0.99985 * jax.random.normal(jax.random.fold_in(_gk, 11), (400000, 3), jnp.float32)
        edge_attr_48 = -3.69585e-06 + 0.999911 * jax.random.normal(jax.random.fold_in(_gk, 12), (400000, 48), jnp.float32)
        return (x, src, dst, edge_attr_3, edge_attr_48)
    x, src, dst, edge_attr_3, edge_attr_48 = _rec_inputs()

    def _L0_gnn_setup():
        import jax, jax.numpy as jnp
        import numpy as np
        NS, NV = (16, 4)
        EPS = 1e-05
        N_NODES, N_EDGES = (5000, 50000)

        def _bn_scalar(x, g, b):
            m = x.mean(0)
            v = ((x - m) ** 2).mean(0)
            return (x - m) / jnp.sqrt(v + EPS) * g + b

        def _seg_mean(x, idx, n):
            s = jax.ops.segment_sum(x, idx, num_segments=n)
            c = jax.ops.segment_sum(jnp.ones((idx.shape[0],), x.dtype), idx, num_segments=n)
            return s / jnp.maximum(c, 1.0)[:, None]

        def _edge_weights(edge_attr, w1, b1, w2, b2):
            h = jax.nn.relu(edge_attr @ w1 + b1)
            return h @ w2 + b2

        def _forward(node_attr, edge_attr, edge_vec, fc0_w1, fc0_b1, fc0_w2, fc0_b2, fc1_w1, fc1_b1, fc1_w2, fc1_b2, bn0_gs, bn0_bs, bn0_gv, bn1_gs, bn1_bs, edge_index):
            N = node_attr.shape[0]
            E = edge_attr.shape[0]
            src, dst = (edge_index[0], edge_index[1])
            rhat = edge_vec / (jnp.linalg.norm(edge_vec, axis=-1, keepdims=True) + 1e-12)
            sh1 = rhat * float(np.sqrt(3.0))
            w = _edge_weights(edge_attr, fc0_w1, fc0_b1, fc0_w2, fc0_b2)
            wa = w[:, :NS * NS].reshape(E, NS, NS)
            wb = w[:, NS * NS:].reshape(E, NS, NV)
            x = node_attr[dst]
            inv = float(1.0 / np.sqrt(NS))
            msg_s = jnp.einsum('ei,eij->ej', x, wa) * inv
            msg_v = jnp.einsum('ei,eij,ec->ejc', x, wb, sh1) * inv
            msg = jnp.concatenate([msg_s, msg_v.reshape(E, NV * 3)], axis=-1)
            out = _seg_mean(msg, src, N)
            s0 = _bn_scalar(out[:, :NS], bn0_gs, bn0_bs)
            v0 = out[:, NS:].reshape(N, NV, 3)
            vn = jnp.sqrt((v0 ** 2).mean(axis=(0, 2)) + EPS)
            v0 = v0 / vn[None, :, None] * bn0_gv[None, :, None]
            w = _edge_weights(edge_attr, fc1_w1, fc1_b1, fc1_w2, fc1_b2)
            wa = w[:, :NS * NS].reshape(E, NS, NS)
            wb = w[:, NS * NS:].reshape(E, NV, NS)
            s = s0[dst]
            v = v0[dst]
            path_a = jnp.einsum('ei,eij->ej', s, wa)
            path_b = jnp.einsum('eic,ec,eij->ej', v, sh1, wb) * float(1.0 / np.sqrt(3.0))
            msg = (path_a + path_b) * float(1.0 / np.sqrt(NS + NV))
            node1 = _seg_mean(msg, src, N)
            return _bn_scalar(node1, bn1_gs, bn1_bs)
        key = jax.random.key(seed)
        ks = jax.random.split(key, 8)
        d = 3 * NS
        wn = NS * NS + NS * NV
        g = lambda k, shape, sc: jax.random.normal(k, shape, jnp.float32) * sc
        return {'node_attr': g(ks[0], (N_NODES, NS), 1.0), 'edge_attr': g(ks[1], (N_EDGES, d), 1.0), 'edge_vec': g(ks[2], (N_EDGES, 3), 1.0), 'fc0_w1': g(ks[3], (d, d), d ** (-0.5)), 'fc0_b1': jnp.zeros((d,), jnp.float32), 'fc0_w2': g(ks[4], (d, wn), d ** (-0.5)), 'fc0_b2': jnp.zeros((wn,), jnp.float32), 'fc1_w1': g(ks[5], (d, d), d ** (-0.5)), 'fc1_b1': jnp.zeros((d,), jnp.float32), 'fc1_w2': g(ks[6], (d, wn), d ** (-0.5)), 'fc1_b2': jnp.zeros((wn,), jnp.float32), 'bn0_gs': jnp.ones((NS,), jnp.float32), 'bn0_bs': jnp.zeros((NS,), jnp.float32), 'bn0_gv': jnp.ones((NV,), jnp.float32), 'bn1_gs': jnp.ones((NS,), jnp.float32), 'bn1_bs': jnp.zeros((NS,), jnp.float32), 'edge_index': jax.random.randint(ks[7], (2, N_EDGES), 0, N_NODES)}
    _L0_gnn_all = _L0_gnn_setup()
    _L0_gnn_in = {k: v for k, v in _L0_gnn_all.items() if k in ('fc0_w1', 'fc0_b1', 'fc0_w2', 'fc0_b2', 'fc1_w1', 'fc1_b1', 'fc1_w2', 'fc1_b2', 'bn0_gs', 'bn0_bs', 'bn0_gv', 'bn1_gs', 'bn1_bs')}
    del _L0_gnn_all

    def _L1_gnn_setup():
        import jax, jax.numpy as jnp
        import numpy as np
        N_NODES = 12500
        N_EDGES = 400000
        FEAT = 16
        HID = 64
        key = jax.random.key(seed)
        ks = jax.random.split(key, 8)
        x = jax.random.normal(ks[0], (N_NODES, FEAT), dtype=jnp.float32)
        edge_index = jax.random.randint(ks[1], (2, N_EDGES), 0, N_NODES, dtype=jnp.int64)
        W1 = jax.random.normal(ks[2], (FEAT, HID), dtype=jnp.float32) * (1.0 / np.sqrt(FEAT))
        b1 = jax.random.normal(ks[3], (HID,), dtype=jnp.float32) * 0.01
        W2 = jax.random.normal(ks[4], (HID, HID), dtype=jnp.float32) * (1.0 / np.sqrt(HID))
        b2 = jax.random.normal(ks[5], (HID,), dtype=jnp.float32) * 0.01
        W3 = jax.random.normal(ks[6], (HID, FEAT), dtype=jnp.float32) * (1.0 / np.sqrt(HID))
        b3 = jax.random.normal(ks[7], (FEAT,), dtype=jnp.float32) * 0.01
        return {'x': x, 'edge_index': edge_index, 'W1': W1, 'b1': b1, 'W2': W2, 'b2': b2, 'W3': W3, 'b3': b3}
    _L1_gnn_all = _L1_gnn_setup()
    _L1_gnn_in = {k: v for k, v in _L1_gnn_all.items() if k in ('W1', 'b1', 'W2', 'b2', 'W3', 'b3')}
    del _L1_gnn_all
    return {'x': x, 'src': src, 'dst': dst, 'edge_attr_3': edge_attr_3, 'edge_attr_48': edge_attr_48, 'L0_gnn_fc0_w1': _L0_gnn_in['fc0_w1'], 'L0_gnn_fc0_b1': _L0_gnn_in['fc0_b1'], 'L0_gnn_fc0_w2': _L0_gnn_in['fc0_w2'], 'L0_gnn_fc0_b2': _L0_gnn_in['fc0_b2'], 'L0_gnn_fc1_w1': _L0_gnn_in['fc1_w1'], 'L0_gnn_fc1_b1': _L0_gnn_in['fc1_b1'], 'L0_gnn_fc1_w2': _L0_gnn_in['fc1_w2'], 'L0_gnn_fc1_b2': _L0_gnn_in['fc1_b2'], 'L0_gnn_bn0_gs': _L0_gnn_in['bn0_gs'], 'L0_gnn_bn0_bs': _L0_gnn_in['bn0_bs'], 'L0_gnn_bn0_gv': _L0_gnn_in['bn0_gv'], 'L0_gnn_bn1_gs': _L0_gnn_in['bn1_gs'], 'L0_gnn_bn1_bs': _L0_gnn_in['bn1_bs'], 'L1_gnn_W1': _L1_gnn_in['W1'], 'L1_gnn_b1': _L1_gnn_in['b1'], 'L1_gnn_W2': _L1_gnn_in['W2'], 'L1_gnn_b2': _L1_gnn_in['b2'], 'L1_gnn_W3': _L1_gnn_in['W3'], 'L1_gnn_b3': _L1_gnn_in['b3']}

def reference(x, src, dst, edge_attr_3, edge_attr_48, L0_gnn_fc0_w1, L0_gnn_fc0_b1, L0_gnn_fc0_w2, L0_gnn_fc0_b2, L0_gnn_fc1_w1, L0_gnn_fc1_b1, L0_gnn_fc1_w2, L0_gnn_fc1_b2, L0_gnn_bn0_gs, L0_gnn_bn0_bs, L0_gnn_bn0_gv, L0_gnn_bn1_gs, L0_gnn_bn1_bs, L1_gnn_W1, L1_gnn_b1, L1_gnn_W2, L1_gnn_b2, L1_gnn_W3, L1_gnn_b3):
    import jax
    import jax.numpy as jnp

    def _L0_gnn_ref(node_attr, edge_attr, edge_vec, fc0_w1, fc0_b1, fc0_w2, fc0_b2, fc1_w1, fc1_b1, fc1_w2, fc1_b2, bn0_gs, bn0_bs, bn0_gv, bn1_gs, bn1_bs, edge_index):
        import jax, jax.numpy as jnp
        import numpy as np
        NS, NV = (16, 4)
        EPS = 1e-05
        N_NODES, N_EDGES = (5000, 50000)

        def _bn_scalar(x, g, b):
            m = x.mean(0)
            v = ((x - m) ** 2).mean(0)
            return (x - m) / jnp.sqrt(v + EPS) * g + b

        def _seg_mean(x, idx, n):
            s = jax.ops.segment_sum(x, idx, num_segments=n)
            c = jax.ops.segment_sum(jnp.ones((idx.shape[0],), x.dtype), idx, num_segments=n)
            return s / jnp.maximum(c, 1.0)[:, None]

        def _edge_weights(edge_attr, w1, b1, w2, b2):
            h = jax.nn.relu(edge_attr @ w1 + b1)
            return h @ w2 + b2

        def _forward(node_attr, edge_attr, edge_vec, fc0_w1, fc0_b1, fc0_w2, fc0_b2, fc1_w1, fc1_b1, fc1_w2, fc1_b2, bn0_gs, bn0_bs, bn0_gv, bn1_gs, bn1_bs, edge_index):
            N = node_attr.shape[0]
            E = edge_attr.shape[0]
            src, dst = (edge_index[0], edge_index[1])
            rhat = edge_vec / (jnp.linalg.norm(edge_vec, axis=-1, keepdims=True) + 1e-12)
            sh1 = rhat * float(np.sqrt(3.0))
            w = _edge_weights(edge_attr, fc0_w1, fc0_b1, fc0_w2, fc0_b2)
            wa = w[:, :NS * NS].reshape(E, NS, NS)
            wb = w[:, NS * NS:].reshape(E, NS, NV)
            x = node_attr[dst]
            inv = float(1.0 / np.sqrt(NS))
            msg_s = jnp.einsum('ei,eij->ej', x, wa) * inv
            msg_v = jnp.einsum('ei,eij,ec->ejc', x, wb, sh1) * inv
            msg = jnp.concatenate([msg_s, msg_v.reshape(E, NV * 3)], axis=-1)
            out = _seg_mean(msg, src, N)
            s0 = _bn_scalar(out[:, :NS], bn0_gs, bn0_bs)
            v0 = out[:, NS:].reshape(N, NV, 3)
            vn = jnp.sqrt((v0 ** 2).mean(axis=(0, 2)) + EPS)
            v0 = v0 / vn[None, :, None] * bn0_gv[None, :, None]
            w = _edge_weights(edge_attr, fc1_w1, fc1_b1, fc1_w2, fc1_b2)
            wa = w[:, :NS * NS].reshape(E, NS, NS)
            wb = w[:, NS * NS:].reshape(E, NV, NS)
            s = s0[dst]
            v = v0[dst]
            path_a = jnp.einsum('ei,eij->ej', s, wa)
            path_b = jnp.einsum('eic,ec,eij->ej', v, sh1, wb) * float(1.0 / np.sqrt(3.0))
            msg = (path_a + path_b) * float(1.0 / np.sqrt(NS + NV))
            node1 = _seg_mean(msg, src, N)
            return _bn_scalar(node1, bn1_gs, bn1_bs)
        return _forward(node_attr, edge_attr, edge_vec, fc0_w1, fc0_b1, fc0_w2, fc0_b2, fc1_w1, fc1_b1, fc1_w2, fc1_b2, bn0_gs, bn0_bs, bn0_gv, bn1_gs, bn1_bs, edge_index)

    def _L1_gnn_ref(x, edge_index, W1, b1, W2, b2, W3, b3):
        import jax, jax.numpy as jnp
        import numpy as np
        N_NODES = 12500
        N_EDGES = 400000
        FEAT = 16
        HID = 64
        N = x.shape[0]
        loops = jnp.arange(N, dtype=edge_index.dtype)
        row = jnp.concatenate([edge_index[0], loops])
        col = jnp.concatenate([edge_index[1], loops])
        deg = jax.ops.segment_sum(jnp.ones_like(col, dtype=x.dtype), col, num_segments=N)
        deg_inv_sqrt = jnp.where(deg > 0, jax.lax.rsqrt(jnp.maximum(deg, 1e-12)), 0.0)
        norm = deg_inv_sqrt[row] * deg_inv_sqrt[col]

        def gcn_layer(h, W, b):
            h = h @ W
            msg = norm[:, None] * h[row]
            agg = jax.ops.segment_sum(msg, col, num_segments=N)
            return agg + b
        h = jax.nn.relu(gcn_layer(x, W1, b1))
        h = jax.nn.relu(gcn_layer(h, W2, b2))
        return gcn_layer(h, W3, b3)
    edge_index = jnp.stack([src, dst])
    x = _layernorm(x + _L0_gnn_ref(x, edge_attr_48, edge_attr_3, L0_gnn_fc0_w1, L0_gnn_fc0_b1, L0_gnn_fc0_w2, L0_gnn_fc0_b2, L0_gnn_fc1_w1, L0_gnn_fc1_b1, L0_gnn_fc1_w2, L0_gnn_fc1_b2, L0_gnn_bn0_gs, L0_gnn_bn0_bs, L0_gnn_bn0_gv, L0_gnn_bn1_gs, L0_gnn_bn1_bs, edge_index), axis=-1)
    x = _layernorm(x + _L1_gnn_ref(x, edge_index, L1_gnn_W1, L1_gnn_b1, L1_gnn_W2, L1_gnn_b2, L1_gnn_W3, L1_gnn_b3), axis=-1)
    return x

_drawn_inputs = setup_inputs


def setup_inputs(seed=0):
    import zlib

    import numpy as np

    out = dict(_drawn_inputs(seed))
    spreads = {'L0_gnn_fc0_b1': (0.0, 0.1),
     'L0_gnn_fc0_b2': (0.0, 0.1),
     'L0_gnn_fc1_b1': (0.0, 0.1),
     'L0_gnn_fc1_b2': (0.0, 0.1),
     'L0_gnn_bn0_gs': (1.0, 0.2),
     'L0_gnn_bn0_bs': (0.0, 0.1),
     'L0_gnn_bn0_gv': (1.0, 0.2),
     'L0_gnn_bn1_gs': (1.0, 0.2),
     'L0_gnn_bn1_bs': (0.0, 0.1)}
    factors = {'L1_gnn_b1': 8.0, 'L1_gnn_b2': 8.0, 'L1_gnn_b3': 6.493}
    for name, (base, spread) in spreads.items():
        noise = np.random.default_rng([zlib.crc32(name.encode()), seed]).standard_normal(out[name].shape)
        drawn = base * np.exp(spread * noise) if base else spread * noise
        out[name] = jnp.asarray(drawn.astype(out[name].dtype))
    for name, factor in factors.items():
        out[name] = (out[name] * factor).astype(out[name].dtype)
    return out
```

```python
from contextlib import ExitStack

import concourse.bass as bass
from concourse import mybir

F32 = mybir.dt.float32
I32 = mybir.dt.int32
ALU = mybir.AluOpType
ACT = mybir.ActivationFunctionType
AX = mybir.AxisListType

N = 12500
E = 400000
P = 128
T = 5
R = 5
GE = P * T
NG = E // GE
ROUNDS = NG // R
W = 32
NP, NA = 125, 100
NS, NV, NC = 16, 4, 3
FE = 48
WN = NS * NS + NS * NV
FT = NS + NV * NC
ACC_ROWS = 99 * P
ACC_F = (32, 16)
HID = 64
CH = 512
NCH = -(-N // CH)
AGG_COLS = NCH * CH
EPS = 1e-5


def at_least(eng, sem, value):
    if not isinstance(value, int) or value > 0:
        eng.wait_ge(sem, value)


def exists(g):
    return not isinstance(g, int) or 0 <= g < NG


def over_groups(eng, step):
    for j in range(R):
        step(0, j)
    with eng.Fori(1, ROUNDS - 1) as s:
        for j in range(R):
            step(s, j)
    for j in range(R):
        step(ROUNDS - 1, j)


def group(s, j, off=0):
    return s * R + (j + off), (j + off) % R, s + ((j + off) // R + 1)


class Scope:

    def __init__(self, nc, stage):
        self.nc, self.stage, self.stack, self.sems = nc, stage, ExitStack(), []

    def __enter__(self):
        return self

    def sb(self, name, shape, dt=F32):
        return self.stack.enter_context(self.nc.sbuf_tensor(f"{self.stage}_{name}", shape, dt))

    def banks(self):
        return [self.stack.enter_context(self.nc.psum_tensor(f"{self.stage}_bank{i}", [P, 512], F32)) for i in range(8)]

    def sem(self, name):
        self.sems.append(self.nc.alloc_semaphore(f"{self.stage}_{name}"))
        return self.sems[-1]

    def __exit__(self, *exc):
        self.stack.close()
        if exc[0] is None:
            self.nc.clear_and_free_semaphores(self.sems)
            self.nc.all_engine_barrier()


def linker(eng, sem):
    count = [0]

    def link(ins):
        count[0] += 1
        ins.then_inc(sem, 1)
        eng.wait_ge(sem, count[0])
    return link


def prepare(nc, d, k):
    with Scope(nc, "prep") as c:
        dst_nat = c.sb("dst_nat", [NP, E // NP], I32)
        ev = c.sb("ev", [NP, E // NP * NC])
        sq = c.sb("sq", [NP, E // NP * NC])
        norm = c.sb("norm", [NP, E // NP])
        rnorm = c.sb("rnorm", [NP, E // NP])
        zeros = c.sb("zeros", [P, ACC_ROWS // P * ACC_F[0]])
        first = c.sb("first", [NP, R])
        basef = c.sb("basef", [NP, R])
        basei = c.sb("basei", [NP, R], I32)
        high = c.sb("high", [NP, R])
        low = c.sb("low", [NP, R])
        over = c.sb("over", [NP, R])
        bad = c.sb("bad", [NP, 1])
        pidx = c.sb("pidx", [P, 1], I32)
        pmod = c.sb("pmod", [P, 1], I32)
        pmodf = c.sb("pmodf", [P, 1])
        iota_w = c.sb("iota_w", [P, W], I32)
        iota_c = c.sb("iota_c", [P, CH], I32)
        ps = c.banks()
        loads, made, cleared, tables_zero = (c.sem(x) for x in ("loads", "made", "cleared", "tables_zero"))
        bases_out, bases_in, norms, units_out = (c.sem(x) for x in ("bases_out", "bases_in", "norms", "units_out"))
        squares, units, bases, bad_ready, bad_sum, dve = (c.sem(x) for x in ("squares", "units", "bases", "bad_ready", "bad_sum", "dve"))
        ev_in = c.sem("ev_in")
        consts = c.sem("consts")
        w1_cleared = c.sem("w1_cleared")
        GP = NG // NP
        assert GP == R

        with nc.Block() as block:
            @block.sync
            def _(sp):
                sp.dma_start(dst_nat[:, :], d["dst_cols"].rearrange("g p t -> (g p t)").rearrange("(q e) -> q e", q=NP)).then_inc(loads, 16)
                sp.dma_start(ev[:, :], d["ev_cols"].rearrange("g p c -> (g p c)").rearrange("(q e) -> q e", q=NP)).then_inc(ev_in, 16)
                sp.wait_ge(w1_cleared, 2)
                for to, of in k["loads"]:
                    sp.dma_start(to, of).then_inc(consts, 16)
                sp.wait_ge(cleared, 1)
                for acc, f in zip(d["acc"], ACC_F):
                    for table in acc:
                        sp.dma_start(table.rearrange("(p a) f -> p (a f)", p=P), zeros[:, 0:ACC_ROWS // P * f]).then_inc(tables_zero, 16)
                sp.wait_ge(bases, 1)
                sp.dma_start(d["base_f"].rearrange("o (q j) -> (o q) j", q=NP), basef[:, :]).then_inc(bases_out, 16)
                sp.dma_start(d["base_i"].rearrange("o (q j) -> (o q) j", q=NP), basei[:, :]).then_inc(bases_out, 16)
                sp.wait_ge(bases_out, 32)
                sp.dma_start(k["base"][:, :], d["base_f"].partition_broadcast(P).rearrange("q o g -> q (o g)")).then_inc(bases_in, 16)
                sp.dma_start(k["base_i"][:, :], d["base_i"]).then_inc(bases_in, 16)
                sp.wait_ge(units, 1)
                sp.dma_start(d["units"].rearrange("g p c -> (g p c)").rearrange("(q e) -> q e", q=NP), sq[:, :]).then_inc(units_out, 16)
                sp.wait_ge(bases_in, 32)
                sp.wait_ge(consts, 16 * len(k["loads"]))
                sp.wait_ge(tables_zero, 16 * sum(len(a) for a in d["acc"]))
                sp.wait_ge(units_out, 16)

            @block.gpsimd
            def _(pool):
                for w1 in k["w1"]:
                    nc.gpsimd.memset(w1[:, :], 0.0).then_inc(w1_cleared, 1)
                nc.gpsimd.memset(zeros[:, :], 0.0).then_inc(cleared, 1)
                nc.gpsimd.memset(k["ones"][:, :], 1.0).then_inc(made, 1)
                nc.gpsimd.memset(k["ident"][:, :], 0.0).then_inc(made, 1)
                nc.gpsimd.iota(pidx[:, :], [[0, 1]], base=0, channel_multiplier=1).then_inc(made, 1)
                nc.gpsimd.iota(iota_w[:, :], [[1, W]], base=0, channel_multiplier=0).then_inc(made, 1)
                nc.gpsimd.iota(iota_c[:, :], [[1, CH]], base=0, channel_multiplier=0).then_inc(made, 1)
                pool.wait_ge(made, 5)
                nc.gpsimd.affine_select(out=k["earlier"][:, :], in_=k["ones"][:, :], compare_op=ALU.is_gt, fill=0.0,
                                        base=0, pattern=[[-1, P]], channel_multiplier=1).then_inc(made, 1)
                nc.gpsimd.affine_select(out=k["ident"][:, :], in_=k["ident"][:, :], compare_op=ALU.not_equal, fill=1.0,
                                        base=0, pattern=[[-1, P]], channel_multiplier=1).then_inc(made, 1)
                pool.wait_ge(made, 7)

            @block.vector
            def _(v):
                link = linker(v, dve)
                v.wait_ge(loads, 16)
                dst_g = dst_nat[:, :].rearrange("q (j e) -> q j e", j=R)
                link(nc.vector.tensor_copy(first[:, :], dst_g[:, :, 0]))
                link(nc.vector.tensor_scalar(basef[:, :], first[:, :], float(N - W), None, ALU.min))
                link(nc.vector.tensor_copy(basei[:, :], basef[:, :]))
                v.sem_inc(bases, 1)
                nc.vector.tensor_reduce(high[:, :], dst_g, AX.X, ALU.max)
                link(nc.vector.tensor_reduce(low[:, :], dst_g, AX.X, ALU.min))
                link(nc.vector.tensor_tensor(high[:, :], high[:, :], basef[:, :], ALU.subtract))
                link(nc.vector.tensor_tensor(low[:, :], low[:, :], basef[:, :], ALU.is_lt))
                link(nc.vector.tensor_scalar(over[:, :], high[:, :], float(W - 1), None, ALU.is_gt))
                link(nc.vector.tensor_tensor(over[:, :], over[:, :], low[:, :], ALU.add))
                nc.vector.tensor_reduce(bad[:, :], over[:, :], AX.X, ALU.add).then_inc(bad_ready, 1)
                v.wait_ge(ev_in, 16)
                link(nc.vector.tensor_tensor(sq[:, :], ev[:, :], ev[:, :], ALU.mult))
                nc.vector.tensor_reduce(norm[:, :], sq[:, :].rearrange("q (e c) -> q e c", c=NC), AX.X, ALU.add).then_inc(squares, 1)
                v.wait_ge(norms, 1)
                link(nc.vector.tensor_scalar(rnorm[:, :], rnorm[:, :], 1e-12, None, ALU.add))
                link(nc.vector.reciprocal(norm[:, :], rnorm[:, :]))
                nc.vector.tensor_tensor(sq[:, :].rearrange("q (e c) -> q e c", c=NC), ev[:, :].rearrange("q (e c) -> q e c", c=NC),
                                        norm[:, :].unsqueeze(2).to_broadcast([NP, E // NP, NC]), ALU.mult).then_inc(units, 1)
                v.wait_ge(made, 7)
                nc.vector.tensor_copy(k["iota_w"][:, :], iota_w[:, :])
                nc.vector.tensor_copy(k["iota_c"][:, :], iota_c[:, :])
                link(nc.vector.tensor_scalar(k["spare"][:, :], pidx[:, :], float(N), None, ALU.add))
                link(nc.vector.tensor_scalar(pmod[:, :], pidx[:, :], W - 1, None, ALU.bitwise_and))
                link(nc.vector.tensor_copy(pmodf[:, :], pmod[:, :]))
                nc.vector.tensor_reduce(k["quad"][:, :], k["ident"][:, :].rearrange("p (q i) -> p q i", q=4), AX.X, ALU.add)
                v.wait_ge(bases_in, 32)
                link(nc.vector.tensor_scalar(k["base_p"][:, :], k["base"][:, :], pmodf[:, 0:1], None, ALU.add))
                v.wait_ge(bad_sum, 1)
                link(nc.vector.tensor_scalar(k["flag"][:, :], ps[0][0:1, 0:1], 1.0, None, ALU.min))

            @block.scalar
            def _(act):
                act.wait_ge(squares, 1)
                nc.scalar.activation(rnorm[:, :], norm[:, :], ACT.Sqrt).then_inc(norms, 1)

            @block.tensor
            def _(pe):
                pe.wait_ge(bad_ready, 1)
                pe.wait_ge(made, 7)
                nc.tensor.matmul(ps[0][0:NP, 0:1], k["ones"][0:NP, 0:NP], bad[:, :], start=True, stop=True).then_inc(bad_sum, 1)


def message_pass(nc, d, k, second, windowed):
    nin, nout = (NS + NV, NS) if second else (NS, NV + NS)
    table = d["between"] if second else d["x"]
    row = FT if second else NS
    acc = d["acc"][second]
    accw = ACC_F[second]
    sent = NS if second else FT + 1
    at = 0 if second else NV
    msgw = NS if second else NV + FT + 1
    w1, w2, b1 = k["w1"][second], k["w2"][second], k["b1"][second]
    nloads = 7 if windowed else 5
    with Scope(nc, f"pass{second}{'w' if windowed else 'g'}") as c:
        ea = c.sb("ea", [FE, R, GE])
        src_row = c.sb("src_row", [P, R, GE], I32)
        src_col = c.sb("src_col", [P, R, T], I32)
        unit = c.sb("unit", [P, R, T, NC])
        dst_q = c.sb("dst_q", [P, R, 2 * P], I32)
        dst_col = c.sb("dst_col", [P, R, T], I32)
        win = c.sb("win", [P, R, row])
        win_q = c.sb("win_q", [P, R, 4, row])
        hot_t = c.sb("hot_t", [P, R, 2 * P])
        xrow = c.sb("xrow", [P, R, T, row])
        vdot = c.sb("vdot", [P, T, NV, NC])
        hT = c.sb("hT", [FE + 1, R, GE])
        apart = c.sb("apart", [P, GE])
        same = c.sb("same", [P, R, GE])
        prod = c.sb("prod", [P, T, nout, nin])
        msg = c.sb("msg", [P, R, T, msgw])
        junk = c.sb("junk", [P, GE])
        dup = c.sb("dup", [P, T])
        delta = c.sb("delta", [P, T])
        shift = c.sb("shift", [P, T])
        idx = c.sb("idx", [P, R, T], I32)
        tot = c.sb("tot", [P, R, T, accw])
        bank = c.banks()
        w_ps, h_ps, mix_ps = bank[0:T], bank[T:T + 2], bank[T + 2]

        loaded = [c.sem(f"loaded{i}") for i in range(R)]
        preset = c.sem("preset")
        hot_ready = c.sem("hot_ready")
        h_made = c.sem("h_made")
        h_ready = c.sem("h_ready")
        x_made = c.sem("x_made")
        x_ready = c.sem("x_ready")
        rows_in = [c.sem(f"rows_in{i}") for i in range(R)]
        w_made = c.sem("w_made")
        w_used = c.sem("w_used")
        sums = c.sem("sums")
        dots = c.sem("dots")
        x_full = c.sem("x_full")
        msg_ready = c.sem("msg_ready")
        apart_ready = c.sem("apart_ready")
        same_ready = c.sem("same_ready")
        dups = c.sem("dups")
        step_a = c.sem("step_a")
        step_b = c.sem("step_b")
        idx_ready = c.sem("idx_ready")
        idx_kept = c.sem("idx_kept")
        tot_made = c.sem("tot_made")
        tot_ready = c.sem("tot_ready")
        landed = [c.sem(f"landed{t}") for t in range(T)]
        landings = c.sem("landings")
        refills = c.sem("refills")
        asked = c.sem("asked")

        with nc.Block() as block:
            @block.sync
            def _(sp):
                def step(s, j):
                    g, slot, turn = group(s, j)
                    if windowed:
                        base = sp.value_load(k["base_i"][0:1, bass.ds(g, 1)], min_val=0, max_val=N - W)
                    if not windowed:
                        at_least(sp, w_used, (g - R + 1) * T)
                    at_least(sp, h_made, g - R + 1)
                    at_least(sp, same_ready, g - R + 1)
                    at_least(sp, idx_ready, g - R + 1)
                    at_least(sp, msg_ready, g - R + 1)
                    if windowed:
                        at_least(sp, x_made, g - R + 1)
                    sp.sem_inc(refills, 1)
                    one = bass.ds(g, 1)
                    sp.dma_start(ea[:, slot, :], d["ea_t"][one].rearrange("o f e -> (o f) e")).then_inc(loaded[slot], 16)
                    if windowed:
                        sp.dma_start(dst_q[:, slot, 0:P], d["dst_rows"][one, 0:4, :].rearrange("o t e -> (o t) e")
                                     .unsqueeze(1).to_broadcast([4, W, P])).then_inc(loaded[slot], 16)
                        sp.dma_start(dst_q[0:W, slot, P:2 * P], d["dst_rows"][one, 4:5, :].rearrange("o t e -> (o t) e")
                                     .to_broadcast([W, P])).then_inc(loaded[slot], 16)
                        sp.dma_start(win[:, slot, :], table[bass.ds(base, W), :]
                                     .unsqueeze(0).to_broadcast([4, W, row])).then_inc(loaded[slot], 16)
                    else:
                        sp.dma_start(dst_col[:, slot, :], d["dst_cols"][one].rearrange("o p t -> (o p) t")).then_inc(loaded[slot], 16)
                    sp.dma_start(src_row[:, slot, :], d["src_rows"][one].rearrange("o t e -> o (t e)")
                                 .to_broadcast([P, GE])).then_inc(loaded[slot], 16)
                    sp.dma_start(src_col[:, slot, :], d["src_cols"][one].rearrange("o p t -> (o p) t")).then_inc(loaded[slot], 16)
                    sp.dma_start(unit[:, slot, :, :], d["units"][one].rearrange("o p c -> (o p) c")).then_inc(loaded[slot], 16)
                over_groups(sp, step)

            @block.gpsimd
            def _(pool):
                nc.gpsimd.memset(hT[:, :, :], 1.0).then_inc(preset, 1)
                nc.gpsimd.memset(msg[:, :, :, :], 1.0).then_inc(preset, 1)
                nc.gpsimd.memset(tot[:, :, :, :], 0.0).then_inc(preset, 1)
                nc.gpsimd.memset(hot_t[:, :, :], 0.0).then_inc(preset, 1)

                def gather(s, j, off):
                    g, slot, turn = group(s, j, off)
                    if not exists(g):
                        return
                    pool.wait_ge(loaded[slot], 16 * nloads * turn)
                    at_least(pool, w_used, (g - R + 1) * T)
                    pool.sem_inc(asked, 1)
                    for t in range(T):
                        pool.indirect_dma_start(xrow[:, slot, t, :], None, table,
                                                bass.IndirectOffsetOnAxis(ap=dst_col[:, slot, t:t + 1], axis=0)
                                                ).then_inc(rows_in[slot], 16)

                def step(s, j):
                    g, slot, turn = group(s, j)
                    if not windowed:
                        gather(s, j, 1)
                    pool.wait_ge(tot_ready, g + 1)
                    pool.wait_ge(idx_ready, g + 1)
                    for t in range(T):
                        if not isinstance(g, int) or g > 0:
                            pool.wait_ge(landed[t], 16 * g)
                            pool.sem_inc(landings, 1)
                        pool.indirect_dma_start(acc[t], bass.IndirectOffsetOnAxis(ap=idx[:, slot, t:t + 1], axis=0),
                                                tot[:, slot, t, :], None, compute_op=ALU.add).then_inc(landed[t], 16)
                if not windowed:
                    gather(0, 0, 0)
                over_groups(pool, step)
                for t in range(T):
                    pool.wait_ge(landed[t], 16 * NG)

            @block.tensor
            def _(pe):
                def front(s, j, off):
                    g, slot, turn = group(s, j, off)
                    if not exists(g):
                        return
                    pe.wait_ge(loaded[slot], 16 * nloads * turn)
                    at_least(pe, h_ready, g)
                    for half in range(2):
                        mm = nc.tensor.matmul(h_ps[half][:, 0:GE // 2], w1[:, :], ea[:, slot, half * GE // 2:(half + 1) * GE // 2],
                                              start=True, stop=True)
                    mm.then_inc(h_made, 1)
                    if windowed:
                        pe.wait_ge(hot_ready, g + 1)
                        at_least(pe, x_ready, g)
                        at_least(pe, tot_ready, g - 2)
                        nc.tensor.matmul(mix_ps[:, 0:4 * row], hot_t[:, slot, 0:P], win_q[:, slot, :, :].rearrange("p q f -> p (q f)"),
                                         start=True, stop=True)
                        nc.tensor.matmul(mix_ps[:, 4 * row:5 * row], hot_t[:, slot, P:2 * P], win[:, slot, :],
                                         start=True, stop=True).then_inc(x_made, 1)

                def weights(s, j):
                    g, slot, turn = group(s, j)
                    pe.wait_ge(h_ready, g + 1)
                    for t in range(T):
                        at_least(pe, w_used, (g - 1) * T + t + 1)
                        nc.tensor.matmul(w_ps[t][:, 0:nin * nout], hT[:, slot, t * P:(t + 1) * P], w2[:, :],
                                         start=True, stop=True).then_inc(w_made, 1)

                def sum_same(s, j, off):
                    g, slot, turn = group(s, j, off)
                    if not exists(g):
                        return
                    pe.wait_ge(same_ready, g + 1)
                    pe.wait_ge(msg_ready, g + 1)
                    at_least(pe, tot_ready, g)
                    if windowed:
                        ahead = g + 3
                        if isinstance(g, int):
                            ahead = min(ahead, NG)
                        pe.wait_ge(x_ready, ahead)
                    for t in range(T):
                        mm = nc.tensor.matmul(mix_ps[:, 256 + t * accw:256 + t * accw + sent], same[:, slot, t * P:(t + 1) * P],
                                              msg[:, slot, t, at:at + sent], start=True, stop=True)
                    mm.then_inc(tot_made, 1)

                pe.wait_ge(preset, 4)
                front(0, 0, 0)

                def step(s, j):
                    front(s, j, 1)
                    weights(s, j)
                    sum_same(s, j, -1)
                over_groups(pe, step)
                sum_same(ROUNDS - 1, R - 1, 0)

            @block.scalar
            def _(act):
                def front(s, j, off):
                    g, slot, turn = group(s, j, off)
                    if not exists(g):
                        return
                    act.wait_ge(h_made, g + 1)
                    at_least(act, w_made, (g - R + 1) * T)
                    for half in range(2):
                        ins = nc.scalar.activation(hT[0:FE, slot, half * GE // 2:(half + 1) * GE // 2], h_ps[half][0:FE, 0:GE // 2],
                                                   ACT.Relu, bias=b1[:, 0:1])
                    ins.then_inc(h_ready, 1)
                    if windowed:
                        act.wait_ge(x_made, g + 1)
                        at_least(act, w_used, (g - R + 1) * T)
                        nc.scalar.activation(xrow[:, slot, :, :].rearrange("p t f -> p (t f)"), mix_ps[:, 0:T * row],
                                             ACT.Copy).then_inc(x_ready, 1)

                def equal(s, j):
                    g, slot, turn = group(s, j)
                    act.wait_ge(loaded[slot], 16 * nloads * turn)
                    at_least(act, same_ready, g)
                    for t in range(T):
                        ins = nc.scalar.activation(apart[:, t * P:(t + 1) * P], src_row[:, slot, t * P:(t + 1) * P], ACT.Abs,
                                                   bias=src_col[:, slot, t:t + 1], scale=-1.0)
                    ins.then_inc(apart_ready, 1)
                    act.wait_ge(apart_ready, g + 1)
                    at_least(act, tot_made, g - R + 1)
                    at_least(act, idx_ready, g - R + 1)
                    nc.scalar.activation(same[:, slot, :], apart[:, :], ACT.Relu, bias=1.0, scale=-1.0).then_inc(same_ready, 1)

                def sums_out(s, j, off):
                    g, slot, turn = group(s, j, off)
                    if not exists(g):
                        return
                    act.wait_ge(tot_made, g + 1)
                    at_least(act, landings, (g - R + 1) * T)
                    nc.scalar.activation(tot[:, slot, :, 0:sent], mix_ps[:, 256:256 + T * accw].rearrange("p (t f) -> p t f", t=T)[:, :, 0:sent],
                                         ACT.Copy).then_inc(tot_ready, 1)

                act.wait_ge(preset, 4)
                front(0, 0, 0)

                def step(s, j):
                    front(s, j, 1)
                    equal(s, j)
                    sums_out(s, j, -1)
                over_groups(act, step)
                sums_out(ROUNDS - 1, R - 1, 0)

            @block.vector
            def _(v):
                def one_hot(s, j, off):
                    g, slot, turn = group(s, j, off)
                    if not windowed or not exists(g):
                        return
                    v.wait_ge(loaded[slot], 16 * nloads * turn)
                    at_least(v, x_made, g - R + 1)
                    nc.vector.tensor_scalar(hot_t[:, slot, 0:P], dst_q[:, slot, 0:P], k["base_p"][:, bass.ds(g, 1)], None, ALU.is_equal)
                    nc.vector.tensor_scalar(hot_t[0:W, slot, P:2 * P], dst_q[0:W, slot, P:2 * P], k["base_p"][0:W, bass.ds(g, 1)],
                                            None, ALU.is_equal)
                    nc.vector.tensor_tensor(win_q[:, slot, :, :], win[:, slot, :].unsqueeze(1).to_broadcast([P, 4, row]),
                                            k["quad"][:, :].unsqueeze(2).to_broadcast([P, 4, row]), ALU.mult).then_inc(hot_ready, 1)

                def rows_wait(g, slot, turn):
                    if windowed:
                        v.wait_ge(x_ready, g + 1)
                    else:
                        v.wait_ge(rows_in[slot], 16 * T * turn)

                def dot(s, j, off):
                    g, slot, turn = group(s, j, off)
                    if not second or not exists(g):
                        return
                    if not windowed:
                        v.wait_ge(loaded[slot], 16 * nloads * turn)
                    rows_wait(g, slot, turn)
                    at_least(v, x_full, g)
                    nc.vector.tensor_tensor(vdot[:, :, :, :], xrow[:, slot, :, NS:FT].rearrange("p t (i c) -> p t i c", c=NC),
                                            unit[:, slot, :, :].unsqueeze(2).to_broadcast([P, T, NV, NC]), ALU.mult).then_inc(dots, 1)
                    v.wait_ge(dots, g + 1)
                    nc.vector.tensor_reduce(xrow[:, slot, :, NS:NS + NV], vdot[:, :, :, :], AX.X, ALU.add).then_inc(x_full, 1)

                def step(s, j):
                    g, slot, turn = group(s, j)
                    if second:
                        v.wait_ge(x_full, g + 1)
                    else:
                        rows_wait(g, slot, turn)
                    at_least(v, sums, g)
                    for t in range(T):
                        v.wait_ge(w_made, g * T + t + 1)
                        nc.vector.tensor_tensor(prod[:, t, :, :], w_ps[t][:, 0:nin * nout].rearrange("p (o i) -> p o i", i=nin),
                                                xrow[:, slot, t, 0:nin].unsqueeze(1).to_broadcast([P, nout, nin]),
                                                ALU.mult).then_inc(w_used, 1)
                    one_hot(s, j, 2)
                    dot(s, j, 1)
                    v.wait_ge(loaded[slot], 16 * nloads * turn)
                    at_least(v, landings, (g - R + 1) * T)
                    if second:
                        nc.vector.tensor_copy(idx[:, slot, :], k["rows"][:, bass.ds(g * T, T)]).then_inc(idx_ready, 1)
                    else:
                        v.wait_ge(same_ready, g + 1)
                        nc.vector.tensor_scalar(delta[:, :], src_col[:, slot, :], -1.0, k["spare"][:, 0:1], ALU.mult, ALU.add)
                        for t in range(T):
                            ins = nc.vector.tensor_tensor_reduce(junk[:, t * P:(t + 1) * P], same[:, slot, t * P:(t + 1) * P], k["earlier"][:, :],
                                                                 1.0, 0.0, ALU.mult, ALU.add, dup[:, t:t + 1])
                        ins.then_inc(dups, 1)
                    v.wait_ge(w_used, (g + 1) * T)
                    at_least(v, tot_made, g - R + 1)
                    nc.vector.tensor_reduce(msg[:, slot, :, 0:nout], prod[:, :, :, :].rearrange("p t o i -> p (t o) i")
                                            .rearrange("p (t o) i -> p t o i", t=T), AX.X, ALU.add).then_inc(sums, 1)
                    if not second:
                        v.wait_ge(dups, g + 1)
                        nc.vector.scalar_tensor_tensor(shift[:, :], dup[:, :], 0.0, delta[:, :], ALU.is_gt, ALU.mult).then_inc(step_a, 1)
                    v.wait_ge(sums, g + 1)
                    if second:
                        v.sem_inc(msg_ready, 1)
                    else:
                        nc.vector.tensor_tensor(msg[:, slot, :, nout:nout + NV * NC].rearrange("p t (i c) -> p t i c", c=NC),
                                                msg[:, slot, :, 0:NV].unsqueeze(3).to_broadcast([P, T, NV, NC]),
                                                unit[:, slot, :, :].unsqueeze(2).to_broadcast([P, T, NV, NC]), ALU.mult).then_inc(msg_ready, 1)
                        v.wait_ge(step_a, g + 1)
                        nc.vector.tensor_tensor(idx[:, slot, :], shift[:, :], src_col[:, slot, :], ALU.add).then_inc(idx_ready, 1)
                        v.wait_ge(idx_ready, g + 1)
                        nc.vector.tensor_copy(k["rows"][:, bass.ds(g * T, T)], idx[:, slot, :]).then_inc(idx_kept, 1)

                v.wait_ge(preset, 4)
                one_hot(0, 0, 0)
                one_hot(0, 1, 0)
                dot(0, 0, 0)
                over_groups(v, step)


def sum_pass(nc, d, k, stage, table, f, windowed):
    agg = k["aggT"]
    nodes = W if windowed else CH
    with Scope(nc, f"sum{stage}{'w' if windowed else 'g'}") as c:
        src_col = c.sb("src_col", [P, R, T], I32)
        dst_col = c.sb("dst_col", [P, R, T], I32)
        rel = c.sb("rel", [P, R, T])
        rows = c.sb("rows_got", [P, R, T, f])
        hot = c.sb("hot", [P, R if windowed else 1, T, nodes])
        bank = c.banks()
        src_in = [c.sem(f"src_in{i}") for i in range(R)]
        dst_in = [c.sem(f"dst_in{i}") for i in range(R)]
        dst_asked = c.sem("dst_asked")
        got = [c.sem(f"got{i}") for i in range(R)]
        refills = c.sem("refills")
        asked = c.sem("asked")
        rel_ready = c.sem("rel_ready")
        hot_ready = c.sem("hot_ready")
        made = c.sem("made")
        added = c.sem("added")
        entered = c.sem("entered")
        emptied = c.sem("emptied")

        with nc.Block() as block:
            @block.sync
            def _(sp):
                def step(s, j):
                    g, slot, turn = group(s, j)
                    one = bass.ds(g, 1)
                    at_least(sp, made if windowed else emptied, g - R + 1)
                    sp.sem_inc(refills, 1)
                    if table is not None:
                        sp.dma_start(src_col[:, slot, :], d["src_cols"][one].rearrange("o p t -> (o p) t")).then_inc(src_in[slot], 16)
                over_groups(sp, step)

            @block.scalar
            def _(act):
                def step(s, j):
                    g, slot, turn = group(s, j)
                    at_least(act, hot_ready if windowed else emptied, g - R + 1)
                    act.sem_inc(dst_asked, 1)
                    act.dma_start(dst_col[:, slot, :], d["dst_cols"][bass.ds(g, 1)].rearrange("o p t -> (o p) t")).then_inc(dst_in[slot], 16)
                over_groups(act, step)

            if table is not None:
                @block.gpsimd
                def _(pool):
                    def step(s, j):
                        g, slot, turn = group(s, j)
                        pool.wait_ge(src_in[slot], 16 * turn)
                        at_least(pool, made if windowed else emptied, g - R + 1)
                        pool.sem_inc(asked, 1)
                        for t in range(T):
                            pool.indirect_dma_start(rows[:, slot, t, :], None, table,
                                                    bass.IndirectOffsetOnAxis(ap=src_col[:, slot, t:t + 1], axis=0)
                                                    ).then_inc(got[slot], 16)
                    over_groups(pool, step)
            else:
                @block.gpsimd
                def _(pool):
                    pool.sem_inc(asked, 1)

            def sum_tiles(out, slot, hot_slot):
                for t in range(T):
                    left = k["ones"][:, 0:f] if table is None else rows[:, slot, t, :]
                    mm = nc.tensor.matmul(out, left, hot[:, hot_slot, t, :], start=(t == 0), stop=(t == T - 1))
                return mm

            if windowed:
                @block.tensor
                def _(pe):
                    def step(s, j):
                        g, slot, turn = group(s, j)
                        pe.wait_ge(hot_ready, g + 1)
                        if table is not None:
                            pe.wait_ge(got[slot], 16 * T * turn)
                        at_least(pe, added, g - R + 1)
                        sum_tiles(bank[slot][0:f, 0:W], slot, slot).then_inc(made, 1)
                    over_groups(pe, step)

                @block.vector
                def _(v):
                    def one_hot(s, j, off):
                        g, slot, turn = group(s, j, off)
                        if not exists(g):
                            return
                        v.wait_ge(dst_in[slot], 16 * turn)
                        nc.vector.tensor_scalar(rel[:, slot, :], dst_col[:, slot, :], k["base"][:, bass.ds(g, 1)], None,
                                                ALU.subtract).then_inc(rel_ready, 1)
                        v.wait_ge(rel_ready, g + 1)
                        at_least(v, made, g - R + 1)
                        nc.vector.tensor_tensor(hot[:, slot, :, :], k["iota_w"][:, :].unsqueeze(1).to_broadcast([P, T, W]),
                                                rel[:, slot, :].unsqueeze(2).to_broadcast([P, T, W]), ALU.is_equal).then_inc(hot_ready, 1)

                    def step(s, j):
                        g, slot, turn = group(s, j)
                        one_hot(s, j, 2)
                        base = v.value_load(k["base_i"][0:1, bass.ds(g, 1)], min_val=0, max_val=N - W)
                        v.wait_ge(made, g + 1)
                        at_least(v, added, g)
                        nc.vector.tensor_tensor(agg[0:f, bass.ds(base, W)], agg[0:f, bass.ds(base, W)], bank[slot][0:f, 0:W],
                                                ALU.add).then_inc(added, 1)
                    one_hot(0, 0, 0)
                    one_hot(0, 1, 0)
                    over_groups(v, step)
            else:
                @block.tensor
                def _(pe):
                    def step(s, j):
                        g, slot, turn = group(s, j)
                        if table is not None:
                            pe.wait_ge(got[slot], 16 * T * turn)
                        pe.sem_inc(entered, 1)
                        with pe.Fori(0, NCH) as ch:
                            pe.wait_ge(hot_ready, g * NCH + ch + 1)
                            sum_tiles(bank[0][0:f, 0:CH], slot, 0).then_inc(made, 1)
                    over_groups(pe, step)

                @block.vector
                def _(v):
                    def step(s, j):
                        g, slot, turn = group(s, j)
                        v.wait_ge(dst_in[slot], 16 * turn)
                        nc.vector.tensor_copy(rel[:, slot, :], dst_col[:, slot, :]).then_inc(rel_ready, 1)
                        with v.Fori(0, NCH) as ch:
                            v.wait_ge(rel_ready, g * (NCH + 1) + ch + 1)
                            nc.vector.tensor_tensor(hot[:, 0, :, :], k["iota_c"][:, :].unsqueeze(1).to_broadcast([P, T, CH]),
                                                    rel[:, slot, :].unsqueeze(2).to_broadcast([P, T, CH]), ALU.is_equal).then_inc(hot_ready, 1)
                            v.wait_ge(hot_ready, g * NCH + ch + 1)
                            nc.vector.tensor_scalar(rel[:, slot, :], rel[:, slot, :], float(-CH), None, ALU.add).then_inc(rel_ready, 1)
                            v.wait_ge(made, g * NCH + ch + 1)
                            cols = bass.ds(ch * CH, CH)
                            nc.vector.tensor_tensor(agg[0:f, cols], agg[0:f, cols], bank[0][0:f, 0:CH], ALU.add).then_inc(added, 1)
                            v.wait_ge(added, g * NCH + ch + 1)
                        v.sem_inc(emptied, 1)
                    over_groups(v, step)


def load_tables(sp, tabs, acc, f, sem):
    for t in range(T):
        sp.dma_start(tabs[:, t, :], acc[t][0:N, :].rearrange("(p a) f -> p (a f)", p=NP)).then_inc(sem[t], 16)


def mean_nodes(nc, d, k):
    f = ACC_F[0]
    with Scope(nc, "means") as c:
        tabs = c.sb("tabs", [NP, T, NA * f])
        total = c.sb("total", [NP, NA, f])
        rs = c.sb("rs", [NP, NA])
        rv = c.sb("rv", [NP, NA])
        dev = c.sb("dev", [NP, NA, NS])
        vec = c.sb("vec", [NP, NA, NV * NC])
        sq = c.sb("sq", [NP, NA, FT])
        part = c.sb("part", [NP, NS + NV])
        mean = c.sb("mean", [NP, NS])
        var = c.sb("var", [NP, NS + NV])
        root = c.sb("root", [NP, NS + NV])
        gain = c.sb("gain", [NP, NS + NV])
        out = c.sb("out_rows", [NP, NA, FT])
        ps = c.banks()
        tab_in = [c.sem(f"tab_in{t}") for t in range(T)]
        dve, sums_ready, sums_total, squares_ready, squares_total, var_ready, root_ready, out_ready, out_stored = (
            c.sem(x) for x in ("dve", "sums_ready", "sums_total", "squares_ready", "squares_total", "var_ready",
                               "root_ready", "out_ready", "out_stored"))
        with nc.Block() as block:
            @block.sync
            def _(sp):
                load_tables(sp, tabs, d["acc"][0], f, tab_in)
                sp.wait_ge(out_ready, 1)
                sp.dma_start(d["between"].rearrange("(p a) f -> p (a f)", p=NP), out[:, :, :].rearrange("p a f -> p (a f)")).then_inc(out_stored, 16)
                sp.wait_ge(out_stored, 16)

            @block.tensor
            def _(pe):
                pe.wait_ge(sums_ready, 1)
                nc.tensor.matmul(ps[0][0:NP, 0:NS], k["ones"][0:NP, 0:NP], part[:, 0:NS], start=True, stop=True).then_inc(sums_total, 1)
                pe.wait_ge(squares_ready, 1)
                nc.tensor.matmul(ps[1][0:NP, 0:NS + NV], k["ones"][0:NP, 0:NP], part[:, :], start=True, stop=True).then_inc(squares_total, 1)

            @block.scalar
            def _(act):
                act.wait_ge(var_ready, 1)
                nc.scalar.activation(root[:, :], var[:, :], ACT.Sqrt).then_inc(root_ready, 1)

            @block.vector
            def _(v):
                link = linker(v, dve)
                flat = total[:, :, :].rearrange("p a f -> p (a f)")
                v.wait_ge(tab_in[0], 16)
                v.wait_ge(tab_in[1], 16)
                link(nc.vector.tensor_tensor(flat, tabs[:, 0, :], tabs[:, 1, :], ALU.add))
                for t in range(2, T):
                    v.wait_ge(tab_in[t], 16)
                    link(nc.vector.tensor_tensor(flat, flat, tabs[:, t, :], ALU.add))
                link(nc.vector.tensor_scalar(rs[:, :], total[:, :, FT], 1.0, None, ALU.max))
                link(nc.vector.reciprocal(k["rcount"][:, :], rs[:, :]))
                nc.vector.tensor_scalar(rs[:, :], k["rcount"][:, :], NS ** -0.5, None, ALU.mult)
                link(nc.vector.tensor_scalar(rv[:, :], k["rcount"][:, :], (3.0 / NS) ** 0.5, None, ALU.mult))
                nc.vector.tensor_tensor(vec[:, :, :], total[:, :, NS:FT], rv[:, :].unsqueeze(2).to_broadcast([NP, NA, NV * NC]), ALU.mult)
                link(nc.vector.tensor_tensor(dev[:, :, :], total[:, :, 0:NS], rs[:, :].unsqueeze(2).to_broadcast([NP, NA, NS]), ALU.mult))
                link(nc.vector.tensor_reduce(part[:, 0:NS], dev[:, :, :].rearrange("p a f -> p f a"), AX.X, ALU.add))
                v.sem_inc(sums_ready, 1)
                v.wait_ge(sums_total, 1)
                link(nc.vector.tensor_scalar(mean[:, :], ps[0][0:NP, 0:NS], 1.0 / N, None, ALU.mult))
                link(nc.vector.tensor_tensor(dev[:, :, :], dev[:, :, :], mean[:, :].unsqueeze(1).to_broadcast([NP, NA, NS]), ALU.subtract))
                nc.vector.tensor_tensor(sq[:, :, 0:NS], dev[:, :, :], dev[:, :, :], ALU.mult)
                link(nc.vector.tensor_tensor(sq[:, :, NS:FT], vec[:, :, :], vec[:, :, :], ALU.mult))
                nc.vector.tensor_reduce(part[:, 0:NS], sq[:, :, 0:NS].rearrange("p a f -> p f a"), AX.X, ALU.add)
                link(nc.vector.tensor_reduce(part[:, NS:NS + NV], sq[:, :, NS:FT].rearrange("p a (i c) -> p i a c", c=NC), AX.XY, ALU.add))
                v.sem_inc(squares_ready, 1)
                v.wait_ge(squares_total, 1)
                nc.vector.tensor_scalar(var[:, 0:NS], ps[1][0:NP, 0:NS], 1.0 / N, EPS, ALU.mult, ALU.add)
                link(nc.vector.tensor_scalar(var[:, NS:NS + NV], ps[1][0:NP, NS:NS + NV], 1.0 / (N * NC), EPS, ALU.mult, ALU.add))
                v.sem_inc(var_ready, 1)
                v.wait_ge(root_ready, 1)
                link(nc.vector.reciprocal(gain[:, :], root[:, :]))
                nc.vector.tensor_tensor(mean[:, :], gain[:, 0:NS], k["bn0_gs"][:, :], ALU.mult)
                link(nc.vector.tensor_tensor(root[:, 0:NV], gain[:, NS:NS + NV], k["bn0_gv"][:, :], ALU.mult))
                nc.vector.tensor_tensor(out[:, :, NS:FT].rearrange("p a (i c) -> p a i c", c=NC), vec[:, :, :].rearrange("p a (i c) -> p a i c", c=NC),
                                        root[:, 0:NV].unsqueeze(1).unsqueeze(3).to_broadcast([NP, NA, NV, NC]), ALU.mult)
                link(nc.vector.tensor_tensor(dev[:, :, :], dev[:, :, :], mean[:, :].unsqueeze(1).to_broadcast([NP, NA, NS]), ALU.mult))
                link(nc.vector.tensor_tensor(out[:, :, 0:NS], dev[:, :, :], k["bn0_bs"][:, :].unsqueeze(1).to_broadcast([NP, NA, NS]), ALU.add))
                v.sem_inc(out_ready, 1)


def layer_norm(nc, v, link, out, y, sq, stat, stat2, root_of):
    wide = lambda a: a.unsqueeze(2).to_broadcast([NP, NA, NS])
    link(nc.vector.tensor_reduce(stat[:, :], y[:, :, :], AX.X, ALU.add))
    link(nc.vector.tensor_scalar(stat[:, :], stat[:, :], 1.0 / NS, None, ALU.mult))
    link(nc.vector.tensor_tensor(y[:, :, :], y[:, :, :], wide(stat[:, :]), ALU.subtract))
    link(nc.vector.tensor_tensor(sq[:, :, :], y[:, :, :], y[:, :, :], ALU.mult))
    link(nc.vector.tensor_reduce(stat[:, :], sq[:, :, :], AX.X, ALU.add))
    link(nc.vector.tensor_scalar(stat[:, :], stat[:, :], 1.0 / NS, EPS, ALU.mult, ALU.add))
    root_of()
    link(nc.vector.reciprocal(stat[:, :], stat2[:, :]))
    link(nc.vector.tensor_tensor(out[:, :, :], y[:, :, :], wide(stat[:, :]), ALU.mult))


def by_node(agg, f, a):
    return agg[0:f, 0:N].rearrange("f (p a) -> f a p", a=NA)[:, a, :]


def transpose_rows(nc, pe, k, ps, rows, f, made, copied):
    for i in range(NA // 4):
        at_least(pe, copied, i - 1)
        for q in range(4):
            mm = nc.tensor.matmul(ps[i % 2][0:f, q * NP:(q + 1) * NP], rows[:, 4 * i + q, :], k["ident"][0:NP, 0:NP], start=True, stop=True)
        mm.then_inc(made, 1)


def copy_transposed(nc, v, k, ps, f, made, copied):
    view = k["aggT"][0:f, 0:N].rearrange("f (p a) -> f a p", a=NA)
    for i in range(NA // 4):
        v.wait_ge(made, i + 1)
        nc.vector.tensor_copy(view[:, 4 * i:4 * i + 4, :], ps[i % 2][0:f, 0:4 * NP].rearrange("f (a p) -> f a p", a=4)).then_inc(copied, 1)


def first_norm(nc, d, k):
    f = ACC_F[1]
    with Scope(nc, "norm") as c:
        tabs = c.sb("tabs", [NP, T, NA * f])
        xin = c.sb("xin", [NP, NA, NS])
        total = c.sb("total", [NP, NA, f])
        sq = c.sb("sq", [NP, NA, NS])
        rs = c.sb("rs", [NP, NA])
        stat = c.sb("stat", [NP, NA])
        stat2 = c.sb("stat2", [NP, NA])
        deg = c.sb("deg", [NP, NA])
        part = c.sb("part", [NP, NS])
        mean = c.sb("mean", [NP, NS])
        rows = c.sb("rows_out", [NP, NA, NS])
        ps = c.banks()
        tab_in = [c.sem(f"tab_in{t}") for t in range(T)]
        dve, x_in, deg_out, deg_in, sums_ready, sums_total, root_asked, root_ready, rows_ready, rows_stored, made, copied = (
            c.sem(x) for x in ("dve", "x_in", "deg_out", "deg_in", "sums_ready", "sums_total", "root_asked", "root_ready",
                               "rows_ready", "rows_stored", "made", "copied"))
        with nc.Block() as block:
            @block.sync
            def _(sp):
                sp.dma_start(d["degree"], k["aggT"][0:1, 0:N]).then_inc(deg_out, 16)
                load_tables(sp, tabs, d["acc"][1], f, tab_in)
                sp.dma_start(xin[:, :, :].rearrange("p a f -> p (a f)"), d["x"].rearrange("(p a) f -> p (a f)", p=NP)).then_inc(x_in, 16)
                sp.wait_ge(deg_out, 16)
                sp.dma_start(deg[:, :], d["degree"].rearrange("o (p a) -> (o p) a", p=NP)).then_inc(deg_in, 16)
                sp.wait_ge(rows_ready, 1)
                sp.dma_start(d["gcn"][0].rearrange("(p a) f -> p (a f)", p=NP), rows[:, :, :].rearrange("p a f -> p (a f)")).then_inc(rows_stored, 16)
                sp.wait_ge(rows_stored, 16)

            @block.tensor
            def _(pe):
                for i in range(2):
                    pe.wait_ge(sums_ready, i + 1)
                    nc.tensor.matmul(ps[2 + i][0:NP, 0:NS], k["ones"][0:NP, 0:NP], part[:, :], start=True, stop=True).then_inc(sums_total, 1)
                pe.wait_ge(rows_ready, 1)
                pe.wait_ge(deg_out, 16)
                transpose_rows(nc, pe, k, ps, rows, NS, made, copied)

            @block.scalar
            def _(act):
                act.wait_ge(root_asked, 1)
                nc.scalar.activation(mean[:, :], part[:, :], ACT.Sqrt).then_inc(root_ready, 1)
                act.wait_ge(root_asked, 2)
                nc.scalar.activation(stat2[:, :], stat[:, :], ACT.Sqrt).then_inc(root_ready, 1)
                act.wait_ge(root_asked, 3)
                nc.scalar.activation(stat2[:, :], stat[:, :], ACT.Sqrt).then_inc(root_ready, 1)

            @block.vector
            def _(v):
                link = linker(v, dve)
                flat = total[:, :, :].rearrange("p a f -> p (a f)")
                wide = lambda a: a.unsqueeze(1).to_broadcast([NP, NA, NS])
                asked = [0]

                def root():
                    asked[0] += 1
                    v.sem_inc(root_asked, 1)
                    v.wait_ge(root_ready, asked[0])
                v.wait_ge(tab_in[0], 16)
                v.wait_ge(tab_in[1], 16)
                link(nc.vector.tensor_tensor(flat, tabs[:, 0, :], tabs[:, 1, :], ALU.add))
                for t in range(2, T):
                    v.wait_ge(tab_in[t], 16)
                    link(nc.vector.tensor_tensor(flat, flat, tabs[:, t, :], ALU.add))
                link(nc.vector.tensor_scalar(rs[:, :], k["rcount"][:, :], (NS + NV) ** -0.5, None, ALU.mult))
                link(nc.vector.tensor_tensor(total[:, :, :], total[:, :, :], rs[:, :].unsqueeze(2).to_broadcast([NP, NA, NS]), ALU.mult))
                link(nc.vector.tensor_reduce(part[:, :], total[:, :, :].rearrange("p a f -> p f a"), AX.X, ALU.add))
                v.sem_inc(sums_ready, 1)
                v.wait_ge(sums_total, 1)
                link(nc.vector.tensor_scalar(mean[:, :], ps[2][0:NP, 0:NS], 1.0 / N, None, ALU.mult))
                link(nc.vector.tensor_tensor(total[:, :, :], total[:, :, :], wide(mean[:, :]), ALU.subtract))
                link(nc.vector.tensor_tensor(sq[:, :, :], total[:, :, :], total[:, :, :], ALU.mult))
                link(nc.vector.tensor_reduce(part[:, :], sq[:, :, :].rearrange("p a f -> p f a"), AX.X, ALU.add))
                v.sem_inc(sums_ready, 1)
                v.wait_ge(sums_total, 2)
                link(nc.vector.tensor_scalar(part[:, :], ps[3][0:NP, 0:NS], 1.0 / N, EPS, ALU.mult, ALU.add))
                root()
                link(nc.vector.reciprocal(part[:, :], mean[:, :]))
                link(nc.vector.tensor_tensor(part[:, :], part[:, :], k["bn1_gs"][:, :], ALU.mult))
                link(nc.vector.tensor_tensor(total[:, :, :], total[:, :, :], wide(part[:, :]), ALU.mult))
                link(nc.vector.tensor_tensor(total[:, :, :], total[:, :, :], wide(k["bn1_bs"][:, :]), ALU.add))
                v.wait_ge(x_in, 16)
                link(nc.vector.tensor_tensor(total[:, :, :], total[:, :, :], xin[:, :, :], ALU.add))
                layer_norm(nc, v, link, k["x1"], total, sq, stat, stat2, root)
                v.wait_ge(deg_in, 16)
                link(nc.vector.tensor_scalar(stat[:, :], deg[:, :], 1.0, 1e-12, ALU.add, ALU.max))
                root()
                link(nc.vector.reciprocal(k["dis"][:, :], stat2[:, :]))
                link(nc.vector.tensor_tensor(rows[:, :, :], k["x1"][:, :, :], k["dis"][:, :].unsqueeze(2).to_broadcast([NP, NA, NS]), ALU.mult))
                v.sem_inc(rows_ready, 1)
                copy_transposed(nc, v, k, ps, NS, made, copied)


def gcn_nodes(nc, d, k, layer):
    fin = (NS, HID)[layer]
    fout = (HID, NS)[layer]
    wts, bias = k["W"][layer], k["b"][layer]
    TB = 4
    NB = NA // TB
    with Scope(nc, f"gcn{layer}") as c:
        hid = c.sb("hid", [NP, NA, HID])
        tmp = c.sb("tmp", [NP, 2, TB, HID])
        hidT = c.sb("hidT", [HID, 2, TB * NP])
        rows = c.sb("rows_out", [NP, NA, NS]) if layer else hid
        ps = c.banks()
        z_made, z_used, turned, turned_out, third_made, third_used, dve, rows_ready, rows_stored, made, copied = (
            c.sem(x) for x in ("z_made", "z_used", "turned", "turned_out", "third_made", "third_used", "dve",
                               "rows_ready", "rows_stored", "made", "copied"))
        hid_ready = c.sem("hid_ready")
        with nc.Block() as block:
            @block.sync
            def _(sp):
                sp.wait_ge(rows_ready, NB)
                sp.dma_start(d["gcn"][layer + 1].rearrange("(p a) f -> p (a f)", p=NP), rows[:, :, :].rearrange("p a f -> p (a f)")).then_inc(rows_stored, 16)
                sp.wait_ge(rows_stored, 16)

            @block.tensor
            def _(pe):
                def third(i):
                    pe.wait_ge(hid_ready, i + 1)
                    at_least(pe, turned_out, i - 1)
                    for q in range(TB):
                        mm = nc.tensor.matmul(ps[2 + i % 2][0:HID, q * NP:(q + 1) * NP], hid[:, i * TB + q, :], k["ident"][0:NP, 0:NP], start=True, stop=True)
                    mm.then_inc(turned, 1)
                    pe.wait_ge(turned_out, i + 1)
                    at_least(pe, rows_ready, i - 1)
                    for q in range(TB):
                        mm = nc.tensor.matmul(ps[4 + i % 2][0:NP, q * NS:(q + 1) * NS], hidT[:, i % 2, q * NP:(q + 1) * NP], k["W"][2][:, :], start=True, stop=True)
                    mm.then_inc(third_made, 1)
                for i in range(NB):
                    at_least(pe, z_used, i - 1)
                    for q in range(TB):
                        mm = nc.tensor.matmul(ps[i % 2][0:NP, q * HID:(q + 1) * HID], by_node(k["aggT"], fin, i * TB + q), wts[:, :], start=True, stop=True)
                    mm.then_inc(z_made, 1)
                    if layer and i > 0:
                        third(i - 1)
                if layer:
                    third(NB - 1)
                pe.wait_ge(rows_ready, NB)
                transpose_rows(nc, pe, k, ps[6:8], rows, fout, made, copied)

            @block.scalar
            def _(act):
                if layer:
                    for i in range(NB):
                        act.wait_ge(turned, i + 1)
                        at_least(act, third_made, i - 1)
                        nc.scalar.activation(hidT[:, i % 2, :], ps[2 + i % 2][0:HID, 0:TB * NP], ACT.Copy).then_inc(turned_out, 1)

            @block.vector
            def _(v):
                link = linker(v, dve)

                def table_rows(i):
                    v.wait_ge(third_made, i + 1)
                    tiles = slice(i * TB, (i + 1) * TB)
                    nc.vector.tensor_tensor(rows[:, tiles, :], ps[4 + i % 2][0:NP, 0:TB * NS].rearrange("p (a f) -> p a f", a=TB),
                                            k["dis"][:, tiles].unsqueeze(2).to_broadcast([NP, TB, NS]), ALU.mult).then_inc(rows_ready, 1)
                for i in range(NB):
                    v.wait_ge(z_made, i + 1)
                    tiles = slice(i * TB, (i + 1) * TB)
                    dis = k["dis"][:, tiles].unsqueeze(2).to_broadcast([NP, TB, HID])
                    b = i % 2
                    ins = nc.vector.tensor_tensor(tmp[:, b, :, :], ps[b][0:NP, 0:TB * HID].rearrange("p (a f) -> p a f", a=TB), dis, ALU.mult)
                    ins.then_inc(z_used, 1)
                    v.wait_ge(z_used, i + 1)
                    link(nc.vector.tensor_tensor(tmp[:, b, :, :], tmp[:, b, :, :], bias[:, :].unsqueeze(1).to_broadcast([NP, TB, HID]), ALU.add))
                    if layer == 0:
                        nc.vector.scalar_tensor_tensor(hid[:, tiles, :], tmp[:, b, :, :], 0.0, dis, ALU.max, ALU.mult).then_inc(rows_ready, 1)
                    else:
                        nc.vector.tensor_scalar(hid[:, tiles, :], tmp[:, b, :, :], 0.0, None, ALU.max).then_inc(hid_ready, 1)
                        if i > 0:
                            table_rows(i - 1)
                if layer:
                    table_rows(NB - 1)
                copy_transposed(nc, v, k, ps[6:8], fout, made, copied)


def last_norm(nc, d, k, out):
    TB = 25
    with Scope(nc, "last") as c:
        y = c.sb("y", [NP, NA, NS])
        sq = c.sb("sq", [NP, NA, NS])
        stat = c.sb("stat", [NP, NA])
        stat2 = c.sb("stat2", [NP, NA])
        ps = c.banks()
        made, dve, root_asked, root_ready, y_ready, stored = (c.sem(x) for x in ("made", "dve", "root_asked", "root_ready", "y_ready", "stored"))
        with nc.Block() as block:
            @block.tensor
            def _(pe):
                for i in range(NA // TB):
                    for q in range(TB):
                        mm = nc.tensor.matmul(ps[i][0:NP, q * NS:(q + 1) * NS], by_node(k["aggT"], NS, i * TB + q), k["ident"][0:NS, 0:NS],
                                              start=True, stop=True)
                    mm.then_inc(made, 1)

            @block.scalar
            def _(act):
                act.wait_ge(root_asked, 1)
                nc.scalar.activation(stat2[:, :], stat[:, :], ACT.Sqrt).then_inc(root_ready, 1)

            @block.vector
            def _(v):
                link = linker(v, dve)
                for i in range(NA // TB):
                    v.wait_ge(made, i + 1)
                    tiles = slice(i * TB, (i + 1) * TB)
                    ins = nc.vector.tensor_tensor(y[:, tiles, :], ps[i][0:NP, 0:TB * NS].rearrange("p (a f) -> p a f", a=TB),
                                                  k["dis"][:, tiles].unsqueeze(2).to_broadcast([NP, TB, NS]), ALU.mult)
                link(ins)
                link(nc.vector.tensor_tensor(y[:, :, :], y[:, :, :], k["b"][2][:, :].unsqueeze(1).to_broadcast([NP, NA, NS]), ALU.add))
                link(nc.vector.tensor_tensor(y[:, :, :], y[:, :, :], k["x1"][:, :, :], ALU.add))

                def root():
                    v.sem_inc(root_asked, 1)
                    v.wait_ge(root_ready, 1)
                layer_norm(nc, v, link, sq, y, sq, stat, stat2, root)
                v.sem_inc(y_ready, 1)

            @block.sync
            def _(sp):
                sp.wait_ge(y_ready, 1)
                sp.dma_start(out.rearrange("(p a) f -> p (a f)", p=NP), sq[:, :, :].rearrange("p a f -> p (a f)")).then_inc(stored, 16)
                sp.wait_ge(stored, 16)


def build(nc, a, out):
    with ExitStack() as top:
        def sb(name, shape, dt=F32):
            return top.enter_context(nc.sbuf_tensor(name, shape, dt))

        def dram(name, shape, dt=F32):
            return nc.dram_tensor(name, shape, dt, kind="Internal").ap()

        d = {x: a[x] for x in ("x", "src_cols", "src_rows", "dst_cols", "dst_rows", "ev_cols", "ea_t")}
        d["acc"] = [[dram(f"acc{p}_{t}", (ACC_ROWS, ACC_F[p])) for t in range(T)] for p in range(2)]
        d["units"] = dram("units", (NG, P, T * NC))
        d["base_f"] = dram("base_f", (1, NG))
        d["base_i"] = dram("base_int", (1, NG), I32)
        d["between"] = dram("between", (N, FT))
        d["degree"] = dram("degree", (1, N))
        d["gcn"] = [dram(f"gcn{i}", (N, f)) for i, f in enumerate((NS, HID, NS))]

        k = {"ones": sb("ones", [P, P]), "ident": sb("ident", [P, P]), "earlier": sb("earlier", [P, P]),
             "iota_w": sb("iota_wf", [P, W]), "iota_c": sb("iota_cf", [P, CH]), "quad": sb("quad", [P, 4]),
             "spare": sb("spare", [P, 1]), "base": sb("base", [P, NG]), "base_p": sb("base_p", [P, NG]),
             "base_i": sb("base_i", [1, NG], I32), "flag": sb("flag", [1, 1], I32), "rows": sb("rows", [P, NG * T], I32),
             "rcount": sb("rcount", [NP, NA]), "x1": sb("x1", [NP, NA, NS]), "dis": sb("dis", [NP, NA]),
             "w1": [sb(f"fc{i}_w1", [FE, P]) for i in range(2)], "w2": [sb(f"fc{i}_w2", [FE + 1, WN]) for i in range(2)],
             "b1": [sb(f"fc{i}_b1", [FE, 1]) for i in range(2)],
             "W": [sb("W1", [NS, HID]), sb("W2", [HID, HID]), sb("W3", [HID, NS])],
             "b": [sb("b1", [NP, HID]), sb("b2", [NP, HID]), sb("b3", [NP, NS])],
             "bn0_gs": sb("bn0_gs", [NP, NS]), "bn0_bs": sb("bn0_bs", [NP, NS]), "bn0_gv": sb("bn0_gv", [NP, NV]),
             "bn1_gs": sb("bn1_gs", [NP, NS]), "bn1_bs": sb("bn1_bs", [NP, NS])}
        row = lambda ap, n: ap.rearrange("(o f) -> o f", o=1).to_broadcast([NP, n])
        k["loads"] = [(k["w1"][i][:, 0:FE], a[f"L0_gnn_fc{i}_w1"]) for i in range(2)]
        k["loads"] += [(k["w2"][i][:, :], a[f"w2_{i}"]) for i in range(2)]
        k["loads"] += [(k["b1"][i][:, :], a[f"L0_gnn_fc{i}_b1"].rearrange("(f o) -> f o", o=1)) for i in range(2)]
        k["loads"] += [(k["W"][i][:, :], a[f"L1_gnn_W{i + 1}"]) for i in range(3)]
        k["loads"] += [(k["b"][i][:, :], row(a[f"L1_gnn_b{i + 1}"], (HID, HID, NS)[i])) for i in range(3)]
        k["loads"] += [(k[x][:, :], row(a[f"L0_gnn_{x}"], NV if x == "bn0_gv" else NS)) for x in ("bn0_gs", "bn0_bs", "bn0_gv", "bn1_gs", "bn1_bs")]

        def either(program):
            flag = nc.values_load(k["flag"][0:1, 0:1], min_val=0, max_val=1)
            with nc.If(flag < 1):
                program(True)
            with nc.Else():
                program(False)

        prepare(nc, d, k)
        either(lambda windowed: message_pass(nc, d, k, 0, windowed))
        mean_nodes(nc, d, k)
        either(lambda windowed: message_pass(nc, d, k, 1, windowed))
        with nc.sbuf_tensor("aggT", [HID, AGG_COLS], F32) as agg:
            k["aggT"] = agg
            with Scope(nc, "zero") as c:
                zeroed = c.sem("zeroed")
                with nc.Block() as block:
                    @block.vector
                    def _(v):
                        nc.vector.memset(agg[:, :], 0.0).then_inc(zeroed, 1)
                        v.wait_ge(zeroed, 1)
            either(lambda windowed: sum_pass(nc, d, k, "deg", None, 1, windowed))
            first_norm(nc, d, k)
            either(lambda windowed: sum_pass(nc, d, k, 0, d["gcn"][0], NS, windowed))
            gcn_nodes(nc, d, k, 0)
            either(lambda windowed: sum_pass(nc, d, k, 1, d["gcn"][1], HID, windowed))
            gcn_nodes(nc, d, k, 1)
            either(lambda windowed: sum_pass(nc, d, k, 2, d["gcn"][2], NS, windowed))
            last_norm(nc, d, k, out)


_WEIGHTS = ["L0_gnn_fc0_w1", "L0_gnn_fc0_b1", "L0_gnn_fc1_w1", "L0_gnn_fc1_b1", "L0_gnn_bn0_gs", "L0_gnn_bn0_bs", "L0_gnn_bn0_gv",
            "L0_gnn_bn1_gs", "L0_gnn_bn1_bs", "L1_gnn_W1", "L1_gnn_b1", "L1_gnn_W2", "L1_gnn_b2", "L1_gnn_W3", "L1_gnn_b3"]


def lay_out(inputs):
    import numpy as np

    arrays = {name: np.ascontiguousarray(inputs[name]) for name in ["x", *_WEIGHTS]}
    for name in ("src", "dst"):
        cols = np.asarray(inputs[name]).reshape(NG, P, T)
        arrays[f"{name}_cols"] = np.ascontiguousarray(cols)
        arrays[f"{name}_rows"] = np.ascontiguousarray(cols.transpose(0, 2, 1))
    arrays["ev_cols"] = np.ascontiguousarray(np.asarray(inputs["edge_attr_3"]).reshape(NG, P, T * NC))
    arrays["ea_t"] = np.ascontiguousarray(np.asarray(inputs["edge_attr_48"]).reshape(NG, P, T, FE).transpose(0, 3, 2, 1)).reshape(NG, FE, GE)
    for i in range(2):
        w = np.concatenate([np.asarray(inputs[f"L0_gnn_fc{i}_w2"]), np.asarray(inputs[f"L0_gnn_fc{i}_b2"])[None]])
        if i == 0:
            scalars = w[:, :NS * NS].reshape(FE + 1, NS, NS).transpose(0, 2, 1)
            vectors = w[:, NS * NS:].reshape(FE + 1, NS, NV).transpose(0, 2, 1)
            w = np.concatenate([vectors, scalars], axis=1)
        else:
            w = w.reshape(FE + 1, NS + NV, NS).transpose(0, 2, 1)
        arrays[f"w2_{i}"] = np.ascontiguousarray(w.reshape(FE + 1, WN))
    return arrays


def kernel(**inputs):
    import concourse.bacc as bacc
    from concourse.bass_utils import run_bass_kernel_spmd

    nc = bacc.Bacc("TRN2", target_bir_lowering=False, num_devices=1)
    arrays = lay_out(inputs)
    a = {name: nc.dram_tensor(f"in_{name}", v.shape, mybir.dt.from_np(v.dtype), kind="ExternalInput").ap() for name, v in arrays.items()}
    out = nc.dram_tensor("out_nodes", (N, NS), F32, kind="ExternalOutput").ap()
    build(nc, a, out)
    r = run_bass_kernel_spmd(nc, [{f"in_{name}": v for name, v in arrays.items()}], core_ids=[0])
    return r.results[0]["out_nodes"]
```

```python
from contextlib import ExitStack

import concourse.bass as bass
from concourse import mybir

F32 = mybir.dt.float32
F32R = mybir.dt.float32r
BF16 = mybir.dt.bfloat16
I32 = mybir.dt.int32
ALU = mybir.AluOpType
ACT = mybir.ActivationFunctionType
AX = mybir.AxisListType

N = 12500
E = 400000
P = 128
T = 5
R = 5
GE = P * T
NG = E // GE
ROUNDS = NG // R
W = 32
NP, NA = 125, 100
NS, NV, NC = 16, 4, 3
FE = 48
WN = NS * NS + NS * NV
FT = NS + NV * NC
ACC_ROWS = 99 * P
ACC_F = (32, 16)
HID = 64
UP, LOW = 3, 64
LOTS = (slice(0, 2), slice(2, T))
HIGH12 = -4096
BITS = 22
NB = -(-P // BITS)
CH = 512
NCH = -(-N // CH)
AGG_COLS = NCH * CH
EPS = 1e-5


HALVES = [(slice(0, LOW), slice(LOW, P), slice(0, UP * P)), (slice(LOW, P), slice(0, LOW), slice(UP * P, GE))]


def at_least(eng, sem, value):
    if not isinstance(value, int) or value > 0:
        eng.wait_ge(sem, value)


def top(ap):
    pairs = ap.bitcast(BF16)
    if len(pairs.shape) == 3:
        return pairs.rearrange("p t (f h) -> p t f h", h=2)[:, :, :, 1]
    return pairs.rearrange("p (f h) -> p f h", h=2)[:, :, 1]


def exists(g):
    return not isinstance(g, int) or 0 <= g < NG


def over_groups(eng, step):
    for j in range(R):
        step(0, j)
    with eng.Fori(1, ROUNDS - 1) as s:
        for j in range(R):
            step(s, j)
    for j in range(R):
        step(ROUNDS - 1, j)


def group(s, j, off=0):
    return s * R + (j + off), (j + off) % R, s + ((j + off) // R + 1)


class Scope:

    def __init__(self, nc, stage):
        self.nc, self.stage, self.stack, self.sems = nc, stage, ExitStack(), []

    def __enter__(self):
        return self

    def sb(self, name, shape, dt=F32):
        return self.stack.enter_context(self.nc.sbuf_tensor(f"{self.stage}_{name}", shape, dt))

    def banks(self, joined=0):
        if joined:
            first = self.stack.enter_context(self.nc.psum_tensor(f"{self.stage}_joined", [P, joined, 512], F32))
            return [first] + [self.stack.enter_context(self.nc.psum_tensor(f"{self.stage}_bank{i}", [P, 512], F32)) for i in range(joined, 8)]
        return [self.stack.enter_context(self.nc.psum_tensor(f"{self.stage}_bank{i}", [P, 512], F32)) for i in range(8)]

    def sem(self, name):
        self.sems.append(self.nc.alloc_semaphore(f"{self.stage}_{name}"))
        return self.sems[-1]

    def __exit__(self, *exc):
        self.stack.close()
        if exc[0] is None:
            self.nc.clear_and_free_semaphores(self.sems)
            self.nc.all_engine_barrier()


def linker(eng, sem):
    count = [0]

    def link(ins):
        count[0] += 1
        ins.then_inc(sem, 1)
        eng.wait_ge(sem, count[0])
    return link


def prepare(nc, d, k):
    with Scope(nc, "prep") as c:
        dst_nat = c.sb("dst_nat", [NP, E // NP], I32)
        ev = c.sb("ev", [NP, E // NP * NC])
        sq = c.sb("sq", [NP, E // NP * NC])
        norm = c.sb("norm", [NP, E // NP])
        rnorm = c.sb("rnorm", [NP, E // NP])
        zeros = c.sb("zeros", [P, ACC_ROWS // P * ACC_F[0]])
        first = c.sb("first", [NP, R])
        basef = c.sb("basef", [NP, R])
        basei = c.sb("basei", [NP, R], I32)
        high = c.sb("high", [NP, R])
        low = c.sb("low", [NP, R])
        over = c.sb("over", [NP, R])
        bad = c.sb("bad", [NP, 1])
        pidx = c.sb("pidx", [P, 1], I32)
        pmod = c.sb("pmod", [P, 1], I32)
        pmodf = c.sb("pmodf", [P, 1])
        iota_w = c.sb("iota_w", [P, W], I32)
        iota_c = c.sb("iota_c", [P, CH], I32)
        w2_masked = c.sb("w2_masked", [P, WN])
        ps = c.banks()
        loads, made, cleared, tables_zero = (c.sem(x) for x in ("loads", "made", "cleared", "tables_zero"))
        bases_out, bases_in, norms, units_out = (c.sem(x) for x in ("bases_out", "bases_in", "norms", "units_out"))
        squares, units, bases, bad_ready, bad_sum, dve = (c.sem(x) for x in ("squares", "units", "bases", "bad_ready", "bad_sum", "dve"))
        ev_in = c.sem("ev_in")
        consts = c.sem("consts")
        w1_cleared = c.sem("w1_cleared")
        GP = NG // NP
        assert GP == R

        with nc.Block() as block:
            @block.sync
            def _(sp):
                sp.dma_start(dst_nat[:, :], d["dst_cols"].rearrange("g p t -> (g p t)").rearrange("(q e) -> q e", q=NP)).then_inc(loads, 16)
                sp.dma_start(ev[:, :], d["ev_cols"].rearrange("g p c -> (g p c)").rearrange("(q e) -> q e", q=NP)).then_inc(ev_in, 16)
                sp.wait_ge(w1_cleared, 4)
                for to, of in k["loads"]:
                    sp.dma_start(to, of).then_inc(consts, 16)
                sp.wait_ge(cleared, 1)
                for acc, f in zip(d["acc"], ACC_F):
                    for table in acc:
                        sp.dma_start(table.rearrange("(p a) f -> p (a f)", p=P), zeros[:, 0:ACC_ROWS // P * f]).then_inc(tables_zero, 16)
                sp.wait_ge(bases, 1)
                sp.dma_start(d["base_f"].rearrange("o (q j) -> (o q) j", q=NP), basef[:, :]).then_inc(bases_out, 16)
                sp.dma_start(d["base_i"].rearrange("o (q j) -> (o q) j", q=NP), basei[:, :]).then_inc(bases_out, 16)
                sp.wait_ge(bases_out, 32)
                sp.dma_start(k["base"][:, :], d["base_f"].partition_broadcast(P).rearrange("q o g -> q (o g)")).then_inc(bases_in, 16)
                sp.dma_start(k["base_i"][:, :], d["base_i"]).then_inc(bases_in, 16)
                sp.wait_ge(units, 1)
                sp.dma_start(d["units"].rearrange("g p c -> (g p c)").rearrange("(q e) -> q e", q=NP), sq[:, :]).then_inc(units_out, 16)
                sp.wait_ge(bases_in, 32)
                sp.wait_ge(consts, 16 * len(k["loads"]))
                sp.wait_ge(tables_zero, 16 * sum(len(a) for a in d["acc"]))
                sp.wait_ge(units_out, 16)

            @block.gpsimd
            def _(pool):
                for w1, b1 in zip(k["w1"], k["b1"]):
                    nc.gpsimd.memset(w1[:, :], 0.0).then_inc(w1_cleared, 1)
                    nc.gpsimd.memset(b1[:, :], 1.0).then_inc(w1_cleared, 1)
                nc.gpsimd.memset(zeros[:, :], 0.0).then_inc(cleared, 1)
                nc.gpsimd.memset(k["ones"][:, :], 1.0).then_inc(made, 1)
                nc.gpsimd.memset(k["ident"][:, :], 0.0).then_inc(made, 1)
                nc.gpsimd.iota(pidx[:, :], [[0, 1]], base=0, channel_multiplier=1).then_inc(made, 1)
                nc.gpsimd.iota(iota_w[:, :], [[1, W]], base=0, channel_multiplier=0).then_inc(made, 1)
                nc.gpsimd.iota(iota_c[:, :], [[1, CH]], base=0, channel_multiplier=0).then_inc(made, 1)
                pool.wait_ge(made, 5)
                nc.gpsimd.affine_select(out=k["ident"][:, :], in_=k["ident"][:, :], compare_op=ALU.not_equal, fill=1.0,
                                        base=0, pattern=[[-1, P]], channel_multiplier=1).then_inc(made, 1)
                pool.wait_ge(made, 6)

            @block.vector
            def _(v):
                link = linker(v, dve)
                v.wait_ge(loads, 16)
                dst_g = dst_nat[:, :].rearrange("q (j e) -> q j e", j=R)
                link(nc.vector.tensor_copy(first[:, :], dst_g[:, :, 0]))
                link(nc.vector.tensor_scalar(basef[:, :], first[:, :], float(N - W), None, ALU.min))
                link(nc.vector.tensor_copy(basei[:, :], basef[:, :]))
                v.sem_inc(bases, 1)
                nc.vector.tensor_reduce(high[:, :], dst_g, AX.X, ALU.max)
                link(nc.vector.tensor_reduce(low[:, :], dst_g, AX.X, ALU.min))
                link(nc.vector.tensor_tensor(high[:, :], high[:, :], basef[:, :], ALU.subtract))
                link(nc.vector.tensor_tensor(low[:, :], low[:, :], basef[:, :], ALU.is_lt))
                link(nc.vector.tensor_scalar(over[:, :], high[:, :], float(W - 1), None, ALU.is_gt))
                link(nc.vector.tensor_tensor(over[:, :], over[:, :], low[:, :], ALU.add))
                nc.vector.tensor_reduce(bad[:, :], over[:, :], AX.X, ALU.add).then_inc(bad_ready, 1)
                v.wait_ge(ev_in, 16)
                link(nc.vector.tensor_tensor(sq[:, :], ev[:, :], ev[:, :], ALU.mult))
                nc.vector.tensor_reduce(norm[:, :], sq[:, :].rearrange("q (e c) -> q e c", c=NC), AX.X, ALU.add).then_inc(squares, 1)
                v.wait_ge(norms, 1)
                link(nc.vector.tensor_scalar(rnorm[:, :], rnorm[:, :], 1e-12, None, ALU.add))
                link(nc.vector.reciprocal(norm[:, :], rnorm[:, :]))
                nc.vector.tensor_tensor(sq[:, :].rearrange("q (e c) -> q e c", c=NC), ev[:, :].rearrange("q (e c) -> q e c", c=NC),
                                        norm[:, :].unsqueeze(2).to_broadcast([NP, E // NP, NC]), ALU.mult).then_inc(units, 1)
                v.wait_ge(made, 6)
                nc.vector.tensor_copy(k["iota_w"][:, :], iota_w[:, :])
                nc.vector.tensor_copy(k["iota_c"][:, :], iota_c[:, :])
                link(nc.vector.tensor_scalar(k["spare"][:, :], pidx[:, :], float(N), None, ALU.add))
                link(nc.vector.tensor_scalar(pmod[:, :], pidx[:, :], W - 1, None, ALU.bitwise_and))
                link(nc.vector.tensor_copy(pmodf[:, :], pmod[:, :]))
                nc.vector.tensor_reduce(k["quad"][:, :], k["ident"][:, :].rearrange("p (q i) -> p q i", q=4), AX.X, ALU.add)
                nc.vector.tensor_reduce(k["fold"][:, :], k["ident"][:, :].rearrange("p (q i) -> p i q", q=4), AX.X, ALU.add)
                link(nc.vector.memset(w2_masked[:, :], 0.0))
                for w2 in k["w2_high"] + k["w2_low"]:
                    ins = nc.vector.tensor_copy(w2[:, :], w2_masked[:, :])
                link(ins)
                v.wait_ge(consts, 16 * len(k["loads"]))
                for i in range(2):
                    for at in (0, LOW):
                        masked = w2_masked[at:at + FE + 1, :]
                        w2, w2_high, w2_low = (k[x][i][at:at + FE + 1, :] for x in ("w2", "w2_high", "w2_low"))
                        link(nc.vector.tensor_scalar(masked.bitcast(I32), w2.bitcast(I32), HIGH12, None, ALU.bitwise_and))
                        nc.vector.tensor_copy(w2_high, masked)
                        link(nc.vector.tensor_tensor(w2_low, w2, masked, ALU.subtract))
                v.wait_ge(bases_in, 32)
                link(nc.vector.tensor_scalar(k["base_p"][:, :], k["base"][:, :], pmodf[:, 0:1], None, ALU.add))
                v.wait_ge(bad_sum, 1)
                link(nc.vector.tensor_scalar(k["flag"][:, :], ps[0][0:1, 0:1], 1.0, None, ALU.min))

            @block.scalar
            def _(act):
                act.wait_ge(squares, 1)
                nc.scalar.activation(rnorm[:, :], norm[:, :], ACT.Sqrt).then_inc(norms, 1)

            @block.tensor
            def _(pe):
                pe.wait_ge(bad_ready, 1)
                pe.wait_ge(made, 6)
                nc.tensor.matmul(ps[0][0:NP, 0:1], k["ones"][0:NP, 0:NP], bad[:, :], start=True, stop=True).then_inc(bad_sum, 1)


def message_pass(nc, d, k, second, windowed):
    nin, nout = (NS + NV, NS) if second else (NS, NV + NS)
    table = d["between"] if second else d["x"]
    row = FT if second else NS
    acc = d["acc"][second]
    accw = ACC_F[second]
    at = 0 if second else NV
    ones_at = nout + NV * NC
    bits_at = at + accw
    real = NS if second else FT
    full = accw if second else accw + NB
    msgw = at + full
    w1, b1 = k["w1"][second], k["b1"][second]
    w2_high, w2_low = k["w2_high"][second], k["w2_low"][second]
    count_dst = second and windowed
    nloads = 5 if windowed else 2
    more_loads = 3 if windowed else 4
    with Scope(nc, f"pass{second}{'w' if windowed else 'g'}") as c:
        ea = c.sb("ea", [P, R, UP * P])
        src_row = c.sb("src_row", [P, R, GE], I32)
        src_col = c.sb("src_col", [P, R, T], I32)
        unit = c.sb("unit", [P, R, T, NC])
        dst_q = c.sb("dst_q", [P, R, 2 * P], I32)
        dst_col = c.sb("dst_col", [P, R, T], I32)
        win = c.sb("win", [P, R, row])
        win_q = c.sb("win_q", [P, R, 4, row])
        off_node = c.sb("off_node", [P, 2 * P])
        hot_t = c.sb("hot_t", [P, R, 2 * P])
        counts = c.sb("counts", [P, R])
        xrow = c.sb("xrow", [P, R, T, row])
        vdot = c.sb("vdot", [P, T, NV, NC])
        hT = c.sb("hT", [P, R, UP * P])
        masked = c.sb("masked", [P, R, UP * P])
        halves = c.sb("halves", [P, R, GE], F32R)
        apart = c.sb("apart", [P, GE])
        same = c.sb("same", [P, R, GE], F32 if second else BF16)
        prod = c.sb("prod", [P, T, nout, nin])
        msg = c.sb("msg", [P, R, T, msgw])
        rest1 = c.sb("rest1", [P, R, T, real])
        rest2 = c.sb("rest2", [P, R, T, real])
        places = c.sb("places", [P, T, NB])
        dup = c.sb("dup", [P, T])
        delta = c.sb("delta", [P, R, T])
        shift = c.sb("shift", [P, T])
        idx = c.sb("idx", [P, R, T], I32)
        tot = c.sb("tot", [P, R, T, full])
        w_ps, h_ps, mix_ps, deg_ps = c.banks(T)

        loaded = [c.sem(f"loaded{i}") for i in range(R)]
        more_loaded = [c.sem(f"more_loaded{i}") for i in range(R)]
        preset = c.sem("preset")
        cleared = c.sem("cleared")
        off_ready = c.sem("off_ready")
        hot_ready = c.sem("hot_ready")
        win_ready = c.sem("win_ready")
        deg_made = c.sem("deg_made")
        deg_added = c.sem("deg_added")
        h_made = c.sem("h_made")
        h_ready = c.sem("h_ready")
        masked_ready = c.sem("masked_ready")
        high_ready = c.sem("high_ready")
        low_ready = c.sem("low_ready")
        x_made = c.sem("x_made")
        x_ready = c.sem("x_ready")
        rows_in = [c.sem(f"rows_in{i}") for i in range(R)]
        w_made = c.sem("w_made")
        w_used = c.sem("w_used")
        rests = c.sem("rests")
        full_ready = c.sem("full_ready")
        sums = c.sem("sums")
        dots = c.sem("dots")
        x_full = c.sem("x_full")
        msg_ready = c.sem("msg_ready")
        apart_ready = c.sem("apart_ready")
        same_ready = c.sem("same_ready")
        places_ready = c.sem("places_ready")
        dups = c.sem("dups")
        shifted = c.sem("shifted")
        idx_ready = c.sem("idx_ready")
        idx_kept = c.sem("idx_kept")
        tot_made = c.sem("tot_made")
        tot_ready = c.sem("tot_ready")
        landed = [c.sem(f"landed{t}") for t in range(T)]
        landings = c.sem("landings")
        more_refills = c.sem("more_refills")
        refills = c.sem("refills")
        asked = c.sem("asked")

        with nc.Block() as block:
            @block.sync
            def _(sp):
                def step(s, j):
                    g, slot, turn = group(s, j)
                    if windowed:
                        base = sp.value_load(k["base_i"][0:1, bass.ds(g, 1)], min_val=0, max_val=N - W)
                    at_least(sp, h_made, g - R + 1)
                    if windowed:
                        at_least(sp, x_made, g - R + 1)
                    sp.sem_inc(refills, 1)
                    one = bass.ds(g, 1)
                    sp.dma_start(ea[0:FE, slot, :], d["ea_t"][one].rearrange("o f e -> (o f) e")[:, 0:UP * P]).then_inc(loaded[slot], 16)
                    sp.dma_start(ea[LOW:LOW + FE, slot, 0:GE - UP * P], d["ea_t"][one].rearrange("o f e -> (o f) e")[:, UP * P:GE]
                                 ).then_inc(loaded[slot], 16)
                    if windowed:
                        sp.dma_start(dst_q[:, slot, 0:P], d["dst_rows"][one, 0:4, :].rearrange("o t e -> (o t) e")
                                     .unsqueeze(1).to_broadcast([4, W, P])).then_inc(loaded[slot], 16)
                        sp.dma_start(dst_q[0:W, slot, P:2 * P], d["dst_rows"][one, 4:5, :].rearrange("o t e -> (o t) e")
                                     .to_broadcast([W, P])).then_inc(loaded[slot], 16)
                        sp.dma_start(win[:, slot, :], table[bass.ds(base, W), :]
                                     .unsqueeze(0).to_broadcast([4, W, row])).then_inc(loaded[slot], 16)
                    if not windowed:
                        at_least(sp, w_used, (g - R + 1) * len(LOTS))
                    at_least(sp, same_ready, g - R + 1)
                    at_least(sp, idx_ready if second else idx_kept, g - R + 1)
                    at_least(sp, x_full if second else msg_ready, g - R + 1)
                    sp.sem_inc(more_refills, 1)
                    if not windowed:
                        sp.dma_start(dst_col[:, slot, :], d["dst_cols"][one].rearrange("o p t -> (o p) t")).then_inc(more_loaded[slot], 16)
                    sp.dma_start(src_row[:, slot, :], d["src_rows"][one].rearrange("o t e -> o (t e)")
                                 .to_broadcast([P, GE])).then_inc(more_loaded[slot], 16)
                    sp.dma_start(src_col[:, slot, :], d["src_cols"][one].rearrange("o p t -> (o p) t")).then_inc(more_loaded[slot], 16)
                    sp.dma_start(unit[:, slot, :, :], d["units"][one].rearrange("o p c -> (o p) c")).then_inc(more_loaded[slot], 16)
                sp.wait_ge(cleared, 2)
                over_groups(sp, step)

            @block.gpsimd
            def _(pool):
                nc.gpsimd.memset(ea[:, :, :], 0.0).then_inc(cleared, 1)
                nc.gpsimd.memset(dst_q[:, :, :], -W - P).then_inc(cleared, 1)

                def gather(s, j, off):
                    g, slot, turn = group(s, j, off)
                    if not exists(g):
                        return
                    pool.wait_ge(more_loaded[slot], 16 * more_loads * turn)
                    at_least(pool, w_used, (g - R + 1) * len(LOTS))
                    pool.sem_inc(asked, 1)
                    for t in range(T):
                        pool.indirect_dma_start(xrow[:, slot, t, :], None, table,
                                                bass.IndirectOffsetOnAxis(ap=dst_col[:, slot, t:t + 1], axis=0)
                                                ).then_inc(rows_in[slot], 16)

                def step(s, j):
                    g, slot, turn = group(s, j)
                    if not windowed:
                        gather(s, j, 1)
                    pool.wait_ge(tot_ready, g + 1)
                    pool.wait_ge(idx_ready, g + 1)
                    for t in range(T):
                        if not isinstance(g, int) or g > 0:
                            pool.wait_ge(landed[t], 16 * g)
                            pool.sem_inc(landings, 1)
                        pool.indirect_dma_start(acc[t], bass.IndirectOffsetOnAxis(ap=idx[:, slot, t:t + 1], axis=0),
                                                tot[:, slot, t, 0:accw], None, compute_op=ALU.add).then_inc(landed[t], 16)
                if not windowed:
                    gather(0, 0, 0)
                over_groups(pool, step)
                for t in range(T):
                    pool.wait_ge(landed[t], 16 * NG)

            @block.tensor
            def _(pe):
                def front(s, j, off):
                    g, slot, turn = group(s, j, off)
                    if not exists(g):
                        return
                    pe.wait_ge(loaded[slot], 16 * nloads * turn)
                    at_least(pe, h_ready, g)
                    nc.tensor.matmul(h_ps[:, 0:UP * P], w1[:, :], ea[:, slot, :], start=True, stop=True).then_inc(h_made, 1)
                    if windowed:
                        pe.wait_ge(hot_ready, g + 1)
                        pe.wait_ge(win_ready, g + 1)
                        at_least(pe, x_ready, g)
                        at_least(pe, tot_ready, g - 2)
                        nc.tensor.matmul(mix_ps[:, 0:4 * row], hot_t[:, slot, 0:P], win_q[:, slot, :, :].rearrange("p q f -> p (q f)"),
                                         start=True, stop=True)
                        nc.tensor.matmul(mix_ps[:, 4 * row:5 * row], hot_t[:, slot, P:2 * P], win[:, slot, :],
                                         start=True, stop=True).then_inc(x_made, 1)

                def weights(s, j):
                    g, slot, turn = group(s, j)
                    pe.wait_ge(low_ready, g + 1)
                    pe.wait_ge(high_ready, g + 1)
                    for t in range(T):
                        for n, lot in enumerate(LOTS):
                            if t == lot.start:
                                at_least(pe, w_used, (g - 1) * len(LOTS) + n + 1)
                        both = halves[0:LOW + FE + 1, slot, t * P:(t + 1) * P]
                        nc.tensor.matmul(w_ps[:, t, 0:nin * nout], both, w2_high[0:LOW + FE + 1, :], start=True, stop=False)
                        nc.tensor.matmul(w_ps[:, t, 0:nin * nout], both, w2_low[0:LOW + FE + 1, :],
                                         start=False, stop=True).then_inc(w_made, 1)

                def count(s, j):
                    g, slot, turn = group(s, j)
                    pe.wait_ge(hot_ready, g + 1)
                    at_least(pe, deg_added, g)
                    nc.tensor.matmul(deg_ps[0:1, 0:W], counts[:, slot:slot + 1], k["fold"][:, :],
                                     start=True, stop=True).then_inc(deg_made, 1)

                def sum_same(s, j, off):
                    g, slot, turn = group(s, j, off)
                    if not exists(g):
                        return
                    if second:
                        pe.wait_ge(sums, (g + 1) * len(LOTS))
                    else:
                        pe.wait_ge(msg_ready, g + 1)
                    pe.wait_ge(same_ready, g + 1)
                    at_least(pe, tot_ready, g)
                    if windowed:
                        ahead = g + 3
                        if isinstance(g, int):
                            ahead = min(ahead, NG)
                        pe.wait_ge(x_ready, ahead)
                    for t in range(T):
                        if second:
                            mm = nc.tensor.matmul(mix_ps[:, 256 + t * full:256 + (t + 1) * full], same[:, slot, t * P:(t + 1) * P],
                                                  msg[:, slot, t, :], start=True, stop=True)
                            continue
                        for n, part in enumerate((msg[:, slot, t, at:at + full], rest1[:, slot, t, :], rest2[:, slot, t, :])):
                            width = full if n == 0 else real
                            mm = nc.tensor.matmul(mix_ps[:, 256 + t * full:256 + t * full + width], same[:, slot, t * P:(t + 1) * P],
                                                  top(part), start=(n == 0), stop=(n == 2))
                    mm.then_inc(tot_made, 1)

                pe.wait_ge(cleared, 2)
                if not second:
                    pe.wait_ge(preset, 3)
                front(0, 0, 0)
                front(0, 1, 0)

                def step(s, j):
                    weights(s, j)
                    sum_same(s, j, -1)
                    if count_dst:
                        count(s, j)
                    front(s, j, 2)
                over_groups(pe, step)
                sum_same(ROUNDS - 1, R - 1, 0)

            @block.scalar
            def _(act):
                def front(s, j, off):
                    g, slot, turn = group(s, j, off)
                    if not exists(g):
                        return
                    act.wait_ge(h_made, g + 1)
                    at_least(act, low_ready, g - R + 1)
                    nc.scalar.activation(hT[:, slot, :], h_ps[:, 0:UP * P], ACT.Relu, bias=b1[:, 0:1]).then_inc(h_ready, 1)
                    if windowed:
                        act.wait_ge(x_made, g + 1)
                        at_least(act, w_used, (g - R + 1) * len(LOTS))
                        nc.scalar.activation(xrow[:, slot, :, :].rearrange("p t f -> p (t f)"), mix_ps[:, 0:T * row],
                                             ACT.Copy).then_inc(x_ready, 1)

                def high_halves(s, j, off):
                    g, slot, turn = group(s, j, off)
                    if not exists(g):
                        return
                    act.wait_ge(masked_ready, g + 1)
                    at_least(act, w_made, (g - R + 1) * T)
                    for own, other, cols in HALVES:
                        high = nc.scalar.activation(halves[own, slot, cols], masked[own, slot, 0:cols.stop - cols.start], ACT.Copy)
                    high.then_inc(high_ready, 1)

                def one_hot(s, j, off):
                    g, slot, turn = group(s, j, off)
                    if not windowed or not exists(g):
                        return
                    act.wait_ge(loaded[slot], 16 * nloads * turn)
                    at_least(act, hot_ready, g)
                    at_least(act, x_made, g - R + 1)
                    if count_dst:
                        at_least(act, deg_made, g - R + 1)
                    nc.scalar.activation(off_node[:, :], dst_q[:, slot, :], ACT.Abs, bias=k["base_p"][:, bass.ds(g, 1)],
                                         scale=-1.0).then_inc(off_ready, 1)
                    act.wait_ge(off_ready, g + 1)
                    nc.scalar.activation(hot_t[:, slot, :], off_node[:, :], ACT.Relu, bias=1.0, scale=-1.0,
                                         accum_out=counts[:, slot:slot + 1] if count_dst else None).then_inc(hot_ready, 1)

                def equal(s, j):
                    g, slot, turn = group(s, j)
                    act.wait_ge(more_loaded[slot], 16 * more_loads * turn)
                    at_least(act, same_ready, g)
                    for t in range(T):
                        ins = nc.scalar.activation(apart[:, t * P:(t + 1) * P], src_row[:, slot, t * P:(t + 1) * P], ACT.Abs,
                                                   bias=src_col[:, slot, t:t + 1], scale=-1.0)
                    ins.then_inc(apart_ready, 1)
                    act.wait_ge(apart_ready, g + 1)
                    at_least(act, tot_made, g - R + 1)
                    if not second:
                        at_least(act, idx_ready, g - R + 1)
                        nc.scalar.activation(delta[:, slot, :], src_col[:, slot, :], ACT.Identity, bias=k["spare"][:, 0:1], scale=-1.0)
                    nc.scalar.activation(same[:, slot, :], apart[:, :], ACT.Relu, bias=1.0, scale=-1.0).then_inc(same_ready, 1)

                def sums_out(s, j, off):
                    g, slot, turn = group(s, j, off)
                    if not exists(g):
                        return
                    act.wait_ge(tot_made, g + 1)
                    at_least(act, landings, (g - R + 1) * T)
                    if not second:
                        at_least(act, idx_ready, g - R + 1)
                    nc.scalar.activation(tot[:, slot, :, :].rearrange("p t f -> p (t f)"), mix_ps[:, 256:256 + T * full],
                                         ACT.Copy).then_inc(tot_ready, 1)

                one_hot(0, 0, 0)
                one_hot(0, 1, 0)
                front(0, 0, 0)
                front(0, 1, 0)
                high_halves(0, 0, 0)

                def step(s, j):
                    one_hot(s, j, 2)
                    sums_out(s, j, -1)
                    high_halves(s, j, 1)
                    equal(s, j)
                    front(s, j, 2)
                over_groups(act, step)
                sums_out(ROUNDS - 1, R - 1, 0)

            @block.vector
            def _(v):
                def window(s, j, off):
                    g, slot, turn = group(s, j, off)
                    if not windowed or not exists(g):
                        return
                    v.wait_ge(loaded[slot], 16 * nloads * turn)
                    at_least(v, x_made, g - R + 1)
                    nc.vector.tensor_tensor(win_q[:, slot, :, :], win[:, slot, :].unsqueeze(1).to_broadcast([P, 4, row]),
                                            k["quad"][:, :].unsqueeze(2).to_broadcast([P, 4, row]), ALU.mult).then_inc(win_ready, 1)

                def degrees(s, j, off):
                    g, slot, turn = group(s, j, off)
                    if not count_dst or not exists(g):
                        return
                    base = v.value_load(k["base_i"][0:1, bass.ds(g, 1)], min_val=0, max_val=N - W)
                    v.wait_ge(deg_made, g + 1)
                    at_least(v, deg_added, g)
                    nodes = k["aggT"][0:1, bass.ds(base, W)]
                    nc.vector.tensor_tensor(nodes, nodes, deg_ps[0:1, 0:W], ALU.add).then_inc(deg_added, 1)

                def rows_to_add(s, j, off, steps=(0, 1, 2, 3)):
                    g, slot, turn = group(s, j, off)
                    if not exists(g):
                        return
                    if 0 in steps:
                        v.wait_ge(tot_ready, g + 1)
                        nc.vector.tensor_tensor(places[:, :, :], tot[:, slot, :, accw:full], k["before"][:, :].unsqueeze(1).to_broadcast([P, T, NB]),
                                                ALU.mult).then_inc(places_ready, 1)
                    if 1 in steps:
                        v.wait_ge(places_ready, g + 1)
                        nc.vector.tensor_reduce(dup[:, :], places[:, :, :], AX.X, ALU.add).then_inc(dups, 1)
                    if 2 in steps:
                        at_least(v, landings, (g - R + 1) * T)
                        v.wait_ge(dups, g + 1)
                        nc.vector.scalar_tensor_tensor(shift[:, :], dup[:, :], k["limit"][:, 0:1], delta[:, slot, :],
                                                       ALU.is_ge, ALU.mult).then_inc(shifted, 1)
                    if 3 in steps:
                        v.wait_ge(shifted, g + 1)
                        nc.vector.tensor_tensor(idx[:, slot, :], shift[:, :], src_col[:, slot, :], ALU.add).then_inc(idx_ready, 1)
                        nc.vector.tensor_tensor(k["rows"][:, bass.ds(g * T, T)], shift[:, :], src_col[:, slot, :], ALU.add).then_inc(idx_kept, 1)

                def kept_rows(s, j):
                    g, slot, turn = group(s, j)
                    at_least(v, landings, (g - R + 1) * T)
                    nc.vector.tensor_copy(idx[:, slot, :], k["rows"][:, bass.ds(g * T, T)]).then_inc(idx_ready, 1)

                def rows_wait(g, slot, turn):
                    if windowed:
                        v.wait_ge(x_ready, g + 1)
                    else:
                        v.wait_ge(rows_in[slot], 16 * T * turn)

                def upper_halves(s, j, off):
                    g, slot, turn = group(s, j, off)
                    if not exists(g):
                        return
                    v.wait_ge(h_ready, g + 1)
                    at_least(v, high_ready, g - R + 1)
                    nc.vector.tensor_scalar(masked[:, slot, :].bitcast(I32), hT[:, slot, :].bitcast(I32), HIGH12, None,
                                            ALU.bitwise_and).then_inc(masked_ready, 1)

                def lower_halves(s, j, off):
                    g, slot, turn = group(s, j, off)
                    if not exists(g):
                        return
                    v.wait_ge(masked_ready, g + 1)
                    at_least(v, w_made, (g - R + 1) * T)
                    for own, other, cols in HALVES:
                        of = slice(0, cols.stop - cols.start)
                        low = nc.vector.tensor_tensor(halves[other, slot, cols], hT[own, slot, of], masked[own, slot, of], ALU.subtract)
                    low.then_inc(low_ready, 1)

                def dot(s, j, off, steps=(0, 1)):
                    g, slot, turn = group(s, j, off)
                    if not second or not exists(g):
                        return
                    if 0 in steps:
                        v.wait_ge(more_loaded[slot], 16 * more_loads * turn)
                        rows_wait(g, slot, turn)
                        at_least(v, x_full, g)
                        nc.vector.tensor_tensor(vdot[:, :, :, :], xrow[:, slot, :, NS:FT].rearrange("p t (i c) -> p t i c", c=NC),
                                                unit[:, slot, :, :].unsqueeze(2).to_broadcast([P, T, NV, NC]), ALU.mult).then_inc(dots, 1)
                    if 1 in steps:
                        v.wait_ge(dots, g + 1)
                        nc.vector.tensor_reduce(xrow[:, slot, :, NS:NS + NV], vdot[:, :, :, :], AX.X, ALU.add).then_inc(x_full, 1)

                def step(s, j):
                    g, slot, turn = group(s, j)
                    degrees(s, j, -1)
                    if second:
                        v.wait_ge(x_full, g + 1)
                    else:
                        rows_wait(g, slot, turn)

                    def multiply(n):
                        lot = LOTS[n]
                        v.wait_ge(w_made, g * T + lot.stop)
                        at_least(v, sums, (g - 1) * len(LOTS) + n + 1)
                        nc.vector.tensor_tensor(prod[:, lot, :, :], w_ps[:, lot, 0:nin * nout].rearrange("p t (o i) -> p t o i", i=nin),
                                                xrow[:, slot, lot, 0:nin].unsqueeze(2).to_broadcast([P, lot.stop - lot.start, nout, nin]),
                                                ALU.mult).then_inc(w_used, 1)

                    def add_up(n):
                        v.wait_ge(w_used, g * len(LOTS) + n + 1)
                        if n == 0:
                            at_least(v, tot_made, g - R + 1)
                        nc.vector.tensor_reduce(msg[:, slot, LOTS[n], 0:nout], prod[:, LOTS[n], :, :], AX.X, ALU.add).then_inc(sums, 1)

                    multiply(0)
                    upper_halves(s, j, 1)
                    window(s, j, 2)
                    multiply(1)
                    lower_halves(s, j, 1)
                    add_up(0)
                    dot(s, j, 1, (0,))
                    add_up(1)
                    dot(s, j, 1, (1,))
                    if second:
                        kept_rows(s, j)
                    else:
                        rows_to_add(s, j, -1, (0,))
                        v.wait_ge(more_loaded[slot], 16 * more_loads * turn)
                        v.wait_ge(sums, (g + 1) * len(LOTS))
                        nc.vector.tensor_tensor(msg[:, slot, :, nout:nout + NV * NC].rearrange("p t (i c) -> p t i c", c=NC),
                                                msg[:, slot, :, 0:NV].unsqueeze(3).to_broadcast([P, T, NV, NC]),
                                                unit[:, slot, :, :].unsqueeze(2).to_broadcast([P, T, NV, NC]), ALU.mult).then_inc(full_ready, 1)
                        rows_to_add(s, j, -1, (1,))
                        v.wait_ge(full_ready, g + 1)
                        message = msg[:, slot, :, at:at + real]
                        nc.vector.tensor_tensor(rest1[:, slot, :, :], message, top(message), ALU.subtract).then_inc(rests, 1)
                        rows_to_add(s, j, -1, (2,))
                        v.wait_ge(rests, g + 1)
                        nc.vector.tensor_tensor(rest2[:, slot, :, :], rest1[:, slot, :, :], top(rest1[:, slot, :, :]), ALU.subtract).then_inc(msg_ready, 1)
                        rows_to_add(s, j, -1, (3,))

                if not second:
                    nc.vector.memset(msg[:, :, :, ones_at:ones_at + 1], 1.0).then_inc(preset, 1)
                    nc.vector.memset(msg[:, :, :, ones_at + 1:bits_at], 0.0).then_inc(preset, 1)
                    for slot in range(R):
                        ins = nc.vector.tensor_copy(msg[:, slot, :, bits_at:msgw], k["powers"][:, :].unsqueeze(1).to_broadcast([P, T, NB]))
                    ins.then_inc(preset, 1)
                window(0, 0, 0)
                window(0, 1, 0)
                upper_halves(0, 0, 0)
                lower_halves(0, 0, 0)
                dot(0, 0, 0)
                over_groups(v, step)
                degrees(ROUNDS - 1, R - 1, 0)
                if not second:
                    rows_to_add(ROUNDS - 1, R - 1, 0)


def sum_pass(nc, d, k, stage, table, f, windowed):
    agg = k["aggT"]
    nodes = W if windowed else CH
    with Scope(nc, f"sum{stage}{'w' if windowed else 'g'}") as c:
        src_col = c.sb("src_col", [P, R, T], I32)
        dst_col = c.sb("dst_col", [P, R, T], I32)
        rel = c.sb("rel", [P, R, T])
        rows = c.sb("rows_got", [P, R, T, f])
        hot = c.sb("hot", [P, R if windowed else 1, T, nodes])
        bank = c.banks()
        src_in = [c.sem(f"src_in{i}") for i in range(R)]
        dst_in = [c.sem(f"dst_in{i}") for i in range(R)]
        dst_asked = c.sem("dst_asked")
        got = [c.sem(f"got{i}") for i in range(R)]
        refills = c.sem("refills")
        asked = c.sem("asked")
        rel_ready = c.sem("rel_ready")
        hot_ready = c.sem("hot_ready")
        made = c.sem("made")
        added = c.sem("added")
        entered = c.sem("entered")
        emptied = c.sem("emptied")

        with nc.Block() as block:
            @block.sync
            def _(sp):
                def step(s, j):
                    g, slot, turn = group(s, j)
                    one = bass.ds(g, 1)
                    at_least(sp, made if windowed else emptied, g - R + 1)
                    sp.sem_inc(refills, 1)
                    if table is not None:
                        sp.dma_start(src_col[:, slot, :], d["src_cols"][one].rearrange("o p t -> (o p) t")).then_inc(src_in[slot], 16)
                over_groups(sp, step)

            @block.scalar
            def _(act):
                def step(s, j):
                    g, slot, turn = group(s, j)
                    at_least(act, hot_ready if windowed else emptied, g - R + 1)
                    act.sem_inc(dst_asked, 1)
                    act.dma_start(dst_col[:, slot, :], d["dst_cols"][bass.ds(g, 1)].rearrange("o p t -> (o p) t")).then_inc(dst_in[slot], 16)
                over_groups(act, step)

            if table is not None:
                @block.gpsimd
                def _(pool):
                    def step(s, j):
                        g, slot, turn = group(s, j)
                        pool.wait_ge(src_in[slot], 16 * turn)
                        at_least(pool, made if windowed else emptied, g - R + 1)
                        pool.sem_inc(asked, 1)
                        for t in range(T):
                            pool.indirect_dma_start(rows[:, slot, t, :], None, table,
                                                    bass.IndirectOffsetOnAxis(ap=src_col[:, slot, t:t + 1], axis=0)
                                                    ).then_inc(got[slot], 16)
                    over_groups(pool, step)
            else:
                @block.gpsimd
                def _(pool):
                    pool.sem_inc(asked, 1)

            def sum_tiles(out, slot, hot_slot):
                for t in range(T):
                    left = k["ones"][:, 0:f] if table is None else rows[:, slot, t, :]
                    mm = nc.tensor.matmul(out, left, hot[:, hot_slot, t, :], start=(t == 0), stop=(t == T - 1))
                return mm

            if windowed:
                @block.tensor
                def _(pe):
                    def step(s, j):
                        g, slot, turn = group(s, j)
                        pe.wait_ge(hot_ready, g + 1)
                        if table is not None:
                            pe.wait_ge(got[slot], 16 * T * turn)
                        at_least(pe, added, g - R + 1)
                        sum_tiles(bank[slot][0:f, 0:W], slot, slot).then_inc(made, 1)
                    over_groups(pe, step)

                @block.vector
                def _(v):
                    def one_hot(s, j, off):
                        g, slot, turn = group(s, j, off)
                        if not exists(g):
                            return
                        v.wait_ge(dst_in[slot], 16 * turn)
                        nc.vector.tensor_scalar(rel[:, slot, :], dst_col[:, slot, :], k["base"][:, bass.ds(g, 1)], None,
                                                ALU.subtract).then_inc(rel_ready, 1)
                        v.wait_ge(rel_ready, g + 1)
                        at_least(v, made, g - R + 1)
                        nc.vector.tensor_tensor(hot[:, slot, :, :], k["iota_w"][:, :].unsqueeze(1).to_broadcast([P, T, W]),
                                                rel[:, slot, :].unsqueeze(2).to_broadcast([P, T, W]), ALU.is_equal).then_inc(hot_ready, 1)

                    def step(s, j):
                        g, slot, turn = group(s, j)
                        one_hot(s, j, 2)
                        base = v.value_load(k["base_i"][0:1, bass.ds(g, 1)], min_val=0, max_val=N - W)
                        v.wait_ge(made, g + 1)
                        at_least(v, added, g)
                        nc.vector.tensor_tensor(agg[0:f, bass.ds(base, W)], agg[0:f, bass.ds(base, W)], bank[slot][0:f, 0:W],
                                                ALU.add).then_inc(added, 1)
                    one_hot(0, 0, 0)
                    one_hot(0, 1, 0)
                    over_groups(v, step)
            else:
                @block.tensor
                def _(pe):
                    def step(s, j):
                        g, slot, turn = group(s, j)
                        if table is not None:
                            pe.wait_ge(got[slot], 16 * T * turn)
                        pe.sem_inc(entered, 1)
                        with pe.Fori(0, NCH) as ch:
                            pe.wait_ge(hot_ready, g * NCH + ch + 1)
                            sum_tiles(bank[0][0:f, 0:CH], slot, 0).then_inc(made, 1)
                    over_groups(pe, step)

                @block.vector
                def _(v):
                    def step(s, j):
                        g, slot, turn = group(s, j)
                        v.wait_ge(dst_in[slot], 16 * turn)
                        nc.vector.tensor_copy(rel[:, slot, :], dst_col[:, slot, :]).then_inc(rel_ready, 1)
                        with v.Fori(0, NCH) as ch:
                            v.wait_ge(rel_ready, g * (NCH + 1) + ch + 1)
                            nc.vector.tensor_tensor(hot[:, 0, :, :], k["iota_c"][:, :].unsqueeze(1).to_broadcast([P, T, CH]),
                                                    rel[:, slot, :].unsqueeze(2).to_broadcast([P, T, CH]), ALU.is_equal).then_inc(hot_ready, 1)
                            v.wait_ge(hot_ready, g * NCH + ch + 1)
                            nc.vector.tensor_scalar(rel[:, slot, :], rel[:, slot, :], float(-CH), None, ALU.add).then_inc(rel_ready, 1)
                            v.wait_ge(made, g * NCH + ch + 1)
                            cols = bass.ds(ch * CH, CH)
                            nc.vector.tensor_tensor(agg[0:f, cols], agg[0:f, cols], bank[0][0:f, 0:CH], ALU.add).then_inc(added, 1)
                            v.wait_ge(added, g * NCH + ch + 1)
                        v.sem_inc(emptied, 1)
                    over_groups(v, step)


def load_tables(sp, tabs, acc, f, sem):
    for t in range(T):
        sp.dma_start(tabs[:, t, :], acc[t][0:N, :].rearrange("(p a) f -> p (a f)", p=NP)).then_inc(sem[t], 16)


def mean_nodes(nc, d, k):
    f = ACC_F[0]
    with Scope(nc, "means") as c:
        tabs = c.sb("tabs", [NP, T, NA * f])
        total = c.sb("total", [NP, NA, f])
        rs = c.sb("rs", [NP, NA])
        rv = c.sb("rv", [NP, NA])
        dev = c.sb("dev", [NP, NA, NS])
        vec = c.sb("vec", [NP, NA, NV * NC])
        sq = c.sb("sq", [NP, NA, FT])
        part = c.sb("part", [NP, NS + NV])
        mean = c.sb("mean", [NP, NS])
        var = c.sb("var", [NP, NS + NV])
        root = c.sb("root", [NP, NS + NV])
        gain = c.sb("gain", [NP, NS + NV])
        out = c.sb("out_rows", [NP, NA, FT])
        ps = c.banks()
        tab_in = [c.sem(f"tab_in{t}") for t in range(T)]
        dve, sums_ready, sums_total, squares_ready, squares_total, var_ready, root_ready, out_ready, out_stored = (
            c.sem(x) for x in ("dve", "sums_ready", "sums_total", "squares_ready", "squares_total", "var_ready",
                               "root_ready", "out_ready", "out_stored"))
        with nc.Block() as block:
            @block.sync
            def _(sp):
                load_tables(sp, tabs, d["acc"][0], f, tab_in)
                sp.wait_ge(out_ready, 1)
                sp.dma_start(d["between"].rearrange("(p a) f -> p (a f)", p=NP), out[:, :, :].rearrange("p a f -> p (a f)")).then_inc(out_stored, 16)
                sp.wait_ge(out_stored, 16)

            @block.tensor
            def _(pe):
                pe.wait_ge(sums_ready, 1)
                nc.tensor.matmul(ps[0][0:NP, 0:NS], k["ones"][0:NP, 0:NP], part[:, 0:NS], start=True, stop=True).then_inc(sums_total, 1)
                pe.wait_ge(squares_ready, 1)
                nc.tensor.matmul(ps[1][0:NP, 0:NS + NV], k["ones"][0:NP, 0:NP], part[:, :], start=True, stop=True).then_inc(squares_total, 1)

            @block.scalar
            def _(act):
                act.wait_ge(var_ready, 1)
                nc.scalar.activation(root[:, :], var[:, :], ACT.Sqrt).then_inc(root_ready, 1)

            @block.vector
            def _(v):
                link = linker(v, dve)
                flat = total[:, :, :].rearrange("p a f -> p (a f)")
                v.wait_ge(tab_in[0], 16)
                v.wait_ge(tab_in[1], 16)
                link(nc.vector.tensor_tensor(flat, tabs[:, 0, :], tabs[:, 1, :], ALU.add))
                for t in range(2, T):
                    v.wait_ge(tab_in[t], 16)
                    link(nc.vector.tensor_tensor(flat, flat, tabs[:, t, :], ALU.add))
                link(nc.vector.tensor_scalar(rs[:, :], total[:, :, FT], 1.0, None, ALU.max))
                link(nc.vector.reciprocal(k["rcount"][:, :], rs[:, :]))
                nc.vector.tensor_scalar(rs[:, :], k["rcount"][:, :], NS ** -0.5, None, ALU.mult)
                link(nc.vector.tensor_scalar(rv[:, :], k["rcount"][:, :], (3.0 / NS) ** 0.5, None, ALU.mult))
                nc.vector.tensor_tensor(vec[:, :, :], total[:, :, NS:FT], rv[:, :].unsqueeze(2).to_broadcast([NP, NA, NV * NC]), ALU.mult)
                link(nc.vector.tensor_tensor(dev[:, :, :], total[:, :, 0:NS], rs[:, :].unsqueeze(2).to_broadcast([NP, NA, NS]), ALU.mult))
                link(nc.vector.tensor_reduce(part[:, 0:NS], dev[:, :, :].rearrange("p a f -> p f a"), AX.X, ALU.add))
                v.sem_inc(sums_ready, 1)
                v.wait_ge(sums_total, 1)
                link(nc.vector.tensor_scalar(mean[:, :], ps[0][0:NP, 0:NS], 1.0 / N, None, ALU.mult))
                link(nc.vector.tensor_tensor(dev[:, :, :], dev[:, :, :], mean[:, :].unsqueeze(1).to_broadcast([NP, NA, NS]), ALU.subtract))
                nc.vector.tensor_tensor(sq[:, :, 0:NS], dev[:, :, :], dev[:, :, :], ALU.mult)
                link(nc.vector.tensor_tensor(sq[:, :, NS:FT], vec[:, :, :], vec[:, :, :], ALU.mult))
                nc.vector.tensor_reduce(part[:, 0:NS], sq[:, :, 0:NS].rearrange("p a f -> p f a"), AX.X, ALU.add)
                link(nc.vector.tensor_reduce(part[:, NS:NS + NV], sq[:, :, NS:FT].rearrange("p a (i c) -> p i a c", c=NC), AX.XY, ALU.add))
                v.sem_inc(squares_ready, 1)
                v.wait_ge(squares_total, 1)
                nc.vector.tensor_scalar(var[:, 0:NS], ps[1][0:NP, 0:NS], 1.0 / N, EPS, ALU.mult, ALU.add)
                link(nc.vector.tensor_scalar(var[:, NS:NS + NV], ps[1][0:NP, NS:NS + NV], 1.0 / (N * NC), EPS, ALU.mult, ALU.add))
                v.sem_inc(var_ready, 1)
                v.wait_ge(root_ready, 1)
                link(nc.vector.reciprocal(gain[:, :], root[:, :]))
                nc.vector.tensor_tensor(mean[:, :], gain[:, 0:NS], k["bn0_gs"][:, :], ALU.mult)
                link(nc.vector.tensor_tensor(root[:, 0:NV], gain[:, NS:NS + NV], k["bn0_gv"][:, :], ALU.mult))
                nc.vector.tensor_tensor(out[:, :, NS:FT].rearrange("p a (i c) -> p a i c", c=NC), vec[:, :, :].rearrange("p a (i c) -> p a i c", c=NC),
                                        root[:, 0:NV].unsqueeze(1).unsqueeze(3).to_broadcast([NP, NA, NV, NC]), ALU.mult)
                link(nc.vector.tensor_tensor(dev[:, :, :], dev[:, :, :], mean[:, :].unsqueeze(1).to_broadcast([NP, NA, NS]), ALU.mult))
                link(nc.vector.tensor_tensor(out[:, :, 0:NS], dev[:, :, :], k["bn0_bs"][:, :].unsqueeze(1).to_broadcast([NP, NA, NS]), ALU.add))
                v.sem_inc(out_ready, 1)


def layer_norm(nc, v, link, out, y, sq, stat, stat2, root_of):
    wide = lambda a: a.unsqueeze(2).to_broadcast([NP, NA, NS])
    link(nc.vector.tensor_reduce(stat[:, :], y[:, :, :], AX.X, ALU.add))
    link(nc.vector.tensor_scalar(stat[:, :], stat[:, :], 1.0 / NS, None, ALU.mult))
    link(nc.vector.tensor_tensor(y[:, :, :], y[:, :, :], wide(stat[:, :]), ALU.subtract))
    link(nc.vector.tensor_tensor(sq[:, :, :], y[:, :, :], y[:, :, :], ALU.mult))
    link(nc.vector.tensor_reduce(stat[:, :], sq[:, :, :], AX.X, ALU.add))
    link(nc.vector.tensor_scalar(stat[:, :], stat[:, :], 1.0 / NS, EPS, ALU.mult, ALU.add))
    root_of()
    link(nc.vector.reciprocal(stat[:, :], stat2[:, :]))
    link(nc.vector.tensor_tensor(out[:, :, :], y[:, :, :], wide(stat[:, :]), ALU.mult))


def by_node(agg, f, a):
    return agg[0:f, 0:N].rearrange("f (p a) -> f a p", a=NA)[:, a, :]


def transpose_rows(nc, pe, k, ps, rows, f, made, copied):
    for i in range(NA // 4):
        at_least(pe, copied, i - 1)
        for q in range(4):
            mm = nc.tensor.matmul(ps[i % 2][0:f, q * NP:(q + 1) * NP], rows[:, 4 * i + q, :], k["ident"][0:NP, 0:NP], start=True, stop=True)
        mm.then_inc(made, 1)


def copy_transposed(nc, v, k, ps, f, made, copied):
    view = k["aggT"][0:f, 0:N].rearrange("f (p a) -> f a p", a=NA)
    for i in range(NA // 4):
        v.wait_ge(made, i + 1)
        nc.vector.tensor_copy(view[:, 4 * i:4 * i + 4, :], ps[i % 2][0:f, 0:4 * NP].rearrange("f (a p) -> f a p", a=4)).then_inc(copied, 1)


def first_norm(nc, d, k):
    f = ACC_F[1]
    with Scope(nc, "norm") as c:
        tabs = c.sb("tabs", [NP, T, NA * f])
        xin = c.sb("xin", [NP, NA, NS])
        total = c.sb("total", [NP, NA, f])
        sq = c.sb("sq", [NP, NA, NS])
        rs = c.sb("rs", [NP, NA])
        stat = c.sb("stat", [NP, NA])
        stat2 = c.sb("stat2", [NP, NA])
        deg = c.sb("deg", [NP, NA])
        part = c.sb("part", [NP, NS])
        mean = c.sb("mean", [NP, NS])
        rows = c.sb("rows_out", [NP, NA, NS])
        ps = c.banks()
        tab_in = [c.sem(f"tab_in{t}") for t in range(T)]
        dve, x_in, deg_out, deg_in, sums_ready, sums_total, root_asked, root_ready, rows_ready, rows_stored, made, copied = (
            c.sem(x) for x in ("dve", "x_in", "deg_out", "deg_in", "sums_ready", "sums_total", "root_asked", "root_ready",
                               "rows_ready", "rows_stored", "made", "copied"))
        with nc.Block() as block:
            @block.sync
            def _(sp):
                sp.dma_start(d["degree"], k["aggT"][0:1, 0:N]).then_inc(deg_out, 16)
                load_tables(sp, tabs, d["acc"][1], f, tab_in)
                sp.dma_start(xin[:, :, :].rearrange("p a f -> p (a f)"), d["x"].rearrange("(p a) f -> p (a f)", p=NP)).then_inc(x_in, 16)
                sp.wait_ge(deg_out, 16)
                sp.dma_start(deg[:, :], d["degree"].rearrange("o (p a) -> (o p) a", p=NP)).then_inc(deg_in, 16)
                sp.wait_ge(rows_ready, 1)
                sp.dma_start(d["gcn"][0].rearrange("(p a) f -> p (a f)", p=NP), rows[:, :, :].rearrange("p a f -> p (a f)")).then_inc(rows_stored, 16)
                sp.wait_ge(rows_stored, 16)

            @block.tensor
            def _(pe):
                for i in range(2):
                    pe.wait_ge(sums_ready, i + 1)
                    nc.tensor.matmul(ps[2 + i][0:NP, 0:NS], k["ones"][0:NP, 0:NP], part[:, :], start=True, stop=True).then_inc(sums_total, 1)
                pe.wait_ge(rows_ready, 1)
                pe.wait_ge(deg_out, 16)
                transpose_rows(nc, pe, k, ps, rows, NS, made, copied)

            @block.scalar
            def _(act):
                act.wait_ge(root_asked, 1)
                nc.scalar.activation(mean[:, :], part[:, :], ACT.Sqrt).then_inc(root_ready, 1)
                act.wait_ge(root_asked, 2)
                nc.scalar.activation(stat2[:, :], stat[:, :], ACT.Sqrt).then_inc(root_ready, 1)
                act.wait_ge(root_asked, 3)
                nc.scalar.activation(stat2[:, :], stat[:, :], ACT.Sqrt).then_inc(root_ready, 1)

            @block.vector
            def _(v):
                link = linker(v, dve)
                flat = total[:, :, :].rearrange("p a f -> p (a f)")
                wide = lambda a: a.unsqueeze(1).to_broadcast([NP, NA, NS])
                asked = [0]

                def root():
                    asked[0] += 1
                    v.sem_inc(root_asked, 1)
                    v.wait_ge(root_ready, asked[0])
                v.wait_ge(tab_in[0], 16)
                v.wait_ge(tab_in[1], 16)
                link(nc.vector.tensor_tensor(flat, tabs[:, 0, :], tabs[:, 1, :], ALU.add))
                for t in range(2, T):
                    v.wait_ge(tab_in[t], 16)
                    link(nc.vector.tensor_tensor(flat, flat, tabs[:, t, :], ALU.add))
                link(nc.vector.tensor_scalar(rs[:, :], k["rcount"][:, :], (NS + NV) ** -0.5, None, ALU.mult))
                link(nc.vector.tensor_tensor(total[:, :, :], total[:, :, :], rs[:, :].unsqueeze(2).to_broadcast([NP, NA, NS]), ALU.mult))
                link(nc.vector.tensor_reduce(part[:, :], total[:, :, :].rearrange("p a f -> p f a"), AX.X, ALU.add))
                v.sem_inc(sums_ready, 1)
                v.wait_ge(sums_total, 1)
                link(nc.vector.tensor_scalar(mean[:, :], ps[2][0:NP, 0:NS], 1.0 / N, None, ALU.mult))
                link(nc.vector.tensor_tensor(total[:, :, :], total[:, :, :], wide(mean[:, :]), ALU.subtract))
                link(nc.vector.tensor_tensor(sq[:, :, :], total[:, :, :], total[:, :, :], ALU.mult))
                link(nc.vector.tensor_reduce(part[:, :], sq[:, :, :].rearrange("p a f -> p f a"), AX.X, ALU.add))
                v.sem_inc(sums_ready, 1)
                v.wait_ge(sums_total, 2)
                link(nc.vector.tensor_scalar(part[:, :], ps[3][0:NP, 0:NS], 1.0 / N, EPS, ALU.mult, ALU.add))
                root()
                link(nc.vector.reciprocal(part[:, :], mean[:, :]))
                link(nc.vector.tensor_tensor(part[:, :], part[:, :], k["bn1_gs"][:, :], ALU.mult))
                link(nc.vector.tensor_tensor(total[:, :, :], total[:, :, :], wide(part[:, :]), ALU.mult))
                link(nc.vector.tensor_tensor(total[:, :, :], total[:, :, :], wide(k["bn1_bs"][:, :]), ALU.add))
                v.wait_ge(x_in, 16)
                link(nc.vector.tensor_tensor(total[:, :, :], total[:, :, :], xin[:, :, :], ALU.add))
                layer_norm(nc, v, link, k["x1"], total, sq, stat, stat2, root)
                v.wait_ge(deg_in, 16)
                link(nc.vector.tensor_scalar(stat[:, :], deg[:, :], 1.0, 1e-12, ALU.add, ALU.max))
                root()
                link(nc.vector.reciprocal(k["dis"][:, :], stat2[:, :]))
                link(nc.vector.tensor_tensor(rows[:, :, :], k["x1"][:, :, :], k["dis"][:, :].unsqueeze(2).to_broadcast([NP, NA, NS]), ALU.mult))
                v.sem_inc(rows_ready, 1)
                copy_transposed(nc, v, k, ps, NS, made, copied)


def gcn_nodes(nc, d, k, layer):
    fin = (NS, HID)[layer]
    fout = (HID, NS)[layer]
    wts, bias = k["W"][layer], k["b"][layer]
    TB = 4
    NB = NA // TB
    with Scope(nc, f"gcn{layer}") as c:
        hid = c.sb("hid", [NP, NA, HID])
        tmp = c.sb("tmp", [NP, 2, TB, HID])
        hidT = c.sb("hidT", [HID, 2, TB * NP])
        rows = c.sb("rows_out", [NP, NA, NS]) if layer else hid
        ps = c.banks()
        z_made, z_used, turned, turned_out, third_made, third_used, dve, rows_ready, rows_stored, made, copied = (
            c.sem(x) for x in ("z_made", "z_used", "turned", "turned_out", "third_made", "third_used", "dve",
                               "rows_ready", "rows_stored", "made", "copied"))
        hid_ready = c.sem("hid_ready")
        with nc.Block() as block:
            @block.sync
            def _(sp):
                sp.wait_ge(rows_ready, NB)
                sp.dma_start(d["gcn"][layer + 1].rearrange("(p a) f -> p (a f)", p=NP), rows[:, :, :].rearrange("p a f -> p (a f)")).then_inc(rows_stored, 16)
                sp.wait_ge(rows_stored, 16)

            @block.tensor
            def _(pe):
                def third(i):
                    pe.wait_ge(hid_ready, i + 1)
                    at_least(pe, turned_out, i - 1)
                    for q in range(TB):
                        mm = nc.tensor.matmul(ps[2 + i % 2][0:HID, q * NP:(q + 1) * NP], hid[:, i * TB + q, :], k["ident"][0:NP, 0:NP], start=True, stop=True)
                    mm.then_inc(turned, 1)
                    pe.wait_ge(turned_out, i + 1)
                    at_least(pe, rows_ready, i - 1)
                    for q in range(TB):
                        mm = nc.tensor.matmul(ps[4 + i % 2][0:NP, q * NS:(q + 1) * NS], hidT[:, i % 2, q * NP:(q + 1) * NP], k["W"][2][:, :], start=True, stop=True)
                    mm.then_inc(third_made, 1)
                for i in range(NB):
                    at_least(pe, z_used, i - 1)
                    for q in range(TB):
                        mm = nc.tensor.matmul(ps[i % 2][0:NP, q * HID:(q + 1) * HID], by_node(k["aggT"], fin, i * TB + q), wts[:, :], start=True, stop=True)
                    mm.then_inc(z_made, 1)
                    if layer and i > 0:
                        third(i - 1)
                if layer:
                    third(NB - 1)
                pe.wait_ge(rows_ready, NB)
                transpose_rows(nc, pe, k, ps[6:8], rows, fout, made, copied)

            @block.scalar
            def _(act):
                if layer:
                    for i in range(NB):
                        act.wait_ge(turned, i + 1)
                        at_least(act, third_made, i - 1)
                        nc.scalar.activation(hidT[:, i % 2, :], ps[2 + i % 2][0:HID, 0:TB * NP], ACT.Copy).then_inc(turned_out, 1)

            @block.vector
            def _(v):
                link = linker(v, dve)

                def table_rows(i):
                    v.wait_ge(third_made, i + 1)
                    tiles = slice(i * TB, (i + 1) * TB)
                    nc.vector.tensor_tensor(rows[:, tiles, :], ps[4 + i % 2][0:NP, 0:TB * NS].rearrange("p (a f) -> p a f", a=TB),
                                            k["dis"][:, tiles].unsqueeze(2).to_broadcast([NP, TB, NS]), ALU.mult).then_inc(rows_ready, 1)
                for i in range(NB):
                    v.wait_ge(z_made, i + 1)
                    tiles = slice(i * TB, (i + 1) * TB)
                    dis = k["dis"][:, tiles].unsqueeze(2).to_broadcast([NP, TB, HID])
                    b = i % 2
                    ins = nc.vector.tensor_tensor(tmp[:, b, :, :], ps[b][0:NP, 0:TB * HID].rearrange("p (a f) -> p a f", a=TB), dis, ALU.mult)
                    ins.then_inc(z_used, 1)
                    v.wait_ge(z_used, i + 1)
                    link(nc.vector.tensor_tensor(tmp[:, b, :, :], tmp[:, b, :, :], bias[:, :].unsqueeze(1).to_broadcast([NP, TB, HID]), ALU.add))
                    if layer == 0:
                        nc.vector.scalar_tensor_tensor(hid[:, tiles, :], tmp[:, b, :, :], 0.0, dis, ALU.max, ALU.mult).then_inc(rows_ready, 1)
                    else:
                        nc.vector.tensor_scalar(hid[:, tiles, :], tmp[:, b, :, :], 0.0, None, ALU.max).then_inc(hid_ready, 1)
                        if i > 0:
                            table_rows(i - 1)
                if layer:
                    table_rows(NB - 1)
                copy_transposed(nc, v, k, ps[6:8], fout, made, copied)


def last_norm(nc, d, k, out):
    TB = 25
    with Scope(nc, "last") as c:
        y = c.sb("y", [NP, NA, NS])
        sq = c.sb("sq", [NP, NA, NS])
        stat = c.sb("stat", [NP, NA])
        stat2 = c.sb("stat2", [NP, NA])
        ps = c.banks()
        made, dve, root_asked, root_ready, y_ready, stored = (c.sem(x) for x in ("made", "dve", "root_asked", "root_ready", "y_ready", "stored"))
        with nc.Block() as block:
            @block.tensor
            def _(pe):
                for i in range(NA // TB):
                    for q in range(TB):
                        mm = nc.tensor.matmul(ps[i][0:NP, q * NS:(q + 1) * NS], by_node(k["aggT"], NS, i * TB + q), k["ident"][0:NS, 0:NS],
                                              start=True, stop=True)
                    mm.then_inc(made, 1)

            @block.scalar
            def _(act):
                act.wait_ge(root_asked, 1)
                nc.scalar.activation(stat2[:, :], stat[:, :], ACT.Sqrt).then_inc(root_ready, 1)

            @block.vector
            def _(v):
                link = linker(v, dve)
                for i in range(NA // TB):
                    v.wait_ge(made, i + 1)
                    tiles = slice(i * TB, (i + 1) * TB)
                    ins = nc.vector.tensor_tensor(y[:, tiles, :], ps[i][0:NP, 0:TB * NS].rearrange("p (a f) -> p a f", a=TB),
                                                  k["dis"][:, tiles].unsqueeze(2).to_broadcast([NP, TB, NS]), ALU.mult)
                link(ins)
                link(nc.vector.tensor_tensor(y[:, :, :], y[:, :, :], k["b"][2][:, :].unsqueeze(1).to_broadcast([NP, NA, NS]), ALU.add))
                link(nc.vector.tensor_tensor(y[:, :, :], y[:, :, :], k["x1"][:, :, :], ALU.add))

                def root():
                    v.sem_inc(root_asked, 1)
                    v.wait_ge(root_ready, 1)
                layer_norm(nc, v, link, sq, y, sq, stat, stat2, root)
                v.sem_inc(y_ready, 1)

            @block.sync
            def _(sp):
                sp.wait_ge(y_ready, 1)
                sp.dma_start(out.rearrange("(p a) f -> p (a f)", p=NP), sq[:, :, :].rearrange("p a f -> p (a f)")).then_inc(stored, 16)
                sp.wait_ge(stored, 16)


def build(nc, a, out):
    with ExitStack() as top:
        def sb(name, shape, dt=F32):
            return top.enter_context(nc.sbuf_tensor(name, shape, dt))

        def dram(name, shape, dt=F32):
            return nc.dram_tensor(name, shape, dt, kind="Internal").ap()

        d = {x: a[x] for x in ("x", "src_cols", "src_rows", "dst_cols", "dst_rows", "ev_cols", "ea_t")}
        d["acc"] = [[dram(f"acc{p}_{t}", (ACC_ROWS, ACC_F[p])) for t in range(T)] for p in range(2)]
        d["units"] = dram("units", (NG, P, T * NC))
        d["base_f"] = dram("base_f", (1, NG))
        d["base_i"] = dram("base_int", (1, NG), I32)
        d["between"] = dram("between", (N, FT))
        d["degree"] = dram("degree", (1, N))
        d["gcn"] = [dram(f"gcn{i}", (N, f)) for i, f in enumerate((NS, HID, NS))]

        k = {"ones": sb("ones", [P, P]), "ident": sb("ident", [P, P]), "fold": sb("fold", [P, W]),
             "powers": sb("powers", [P, NB]), "before": sb("before", [P, NB]), "limit": sb("limit", [P, 1]),
             "iota_w": sb("iota_wf", [P, W]), "iota_c": sb("iota_cf", [P, CH]), "quad": sb("quad", [P, 4]),
             "spare": sb("spare", [P, 1]), "base": sb("base", [P, NG]), "base_p": sb("base_p", [P, NG]),
             "base_i": sb("base_i", [1, NG], I32), "flag": sb("flag", [1, 1], I32), "rows": sb("rows", [P, NG * T], I32),
             "rcount": sb("rcount", [NP, NA]), "x1": sb("x1", [NP, NA, NS]), "dis": sb("dis", [NP, NA]),
             "w1": [sb(f"fc{i}_w1", [P, P]) for i in range(2)], "w2": [sb(f"fc{i}_w2", [P, WN]) for i in range(2)],
             "w2_high": [sb(f"fc{i}_w2_high", [P, WN], F32R) for i in range(2)], "w2_low": [sb(f"fc{i}_w2_low", [P, WN], F32R) for i in range(2)],
             "b1": [sb(f"fc{i}_b1", [P, 1]) for i in range(2)],
             "W": [sb("W1", [NS, HID]), sb("W2", [HID, HID]), sb("W3", [HID, NS])],
             "b": [sb("b1", [NP, HID]), sb("b2", [NP, HID]), sb("b3", [NP, NS])],
             "bn0_gs": sb("bn0_gs", [NP, NS]), "bn0_bs": sb("bn0_bs", [NP, NS]), "bn0_gv": sb("bn0_gv", [NP, NV]),
             "bn1_gs": sb("bn1_gs", [NP, NS]), "bn1_bs": sb("bn1_bs", [NP, NS])}
        row = lambda ap, n: ap.rearrange("(o f) -> o f", o=1).to_broadcast([NP, n])
        k["loads"] = [(k["w1"][i][at:at + FE, at:at + FE], a[f"L0_gnn_fc{i}_w1"]) for i in range(2) for at in (0, LOW)]
        k["loads"] += [(k["w2"][i][at:at + FE + 1, :], a[f"w2_{i}"]) for i in range(2) for at in (0, LOW)]
        k["loads"] += [(k["b1"][i][at:at + FE, :], a[f"L0_gnn_fc{i}_b1"].rearrange("(f o) -> f o", o=1)) for i in range(2) for at in (0, LOW)]
        k["loads"] += [(k[x][:, :], a[x]) for x in ("powers", "before", "limit")]
        k["loads"] += [(k["W"][i][:, :], a[f"L1_gnn_W{i + 1}"]) for i in range(3)]
        k["loads"] += [(k["b"][i][:, :], row(a[f"L1_gnn_b{i + 1}"], (HID, HID, NS)[i])) for i in range(3)]
        k["loads"] += [(k[x][:, :], row(a[f"L0_gnn_{x}"], NV if x == "bn0_gv" else NS)) for x in ("bn0_gs", "bn0_bs", "bn0_gv", "bn1_gs", "bn1_bs")]

        def either(program):
            flag = nc.values_load(k["flag"][0:1, 0:1], min_val=0, max_val=1)
            with nc.If(flag < 1):
                program(True)
            with nc.Else():
                program(False)

        prepare(nc, d, k)
        either(lambda windowed: message_pass(nc, d, k, 0, windowed))
        mean_nodes(nc, d, k)
        with nc.sbuf_tensor("aggT", [HID, AGG_COLS], F32) as agg:
            k["aggT"] = agg
            with Scope(nc, "zero") as c:
                zeroed = c.sem("zeroed")
                with nc.Block() as block:
                    @block.vector
                    def _(v):
                        nc.vector.memset(agg[:, :], 0.0).then_inc(zeroed, 1)
                        v.wait_ge(zeroed, 1)

            def second_pass(windowed):
                message_pass(nc, d, k, 1, windowed)
                if not windowed:
                    sum_pass(nc, d, k, "deg", None, 1, False)
            either(second_pass)
            first_norm(nc, d, k)
            either(lambda windowed: sum_pass(nc, d, k, 0, d["gcn"][0], NS, windowed))
            gcn_nodes(nc, d, k, 0)
            either(lambda windowed: sum_pass(nc, d, k, 1, d["gcn"][1], HID, windowed))
            gcn_nodes(nc, d, k, 1)
            either(lambda windowed: sum_pass(nc, d, k, 2, d["gcn"][2], NS, windowed))
            last_norm(nc, d, k, out)


_WEIGHTS = ["L0_gnn_fc0_w1", "L0_gnn_fc0_b1", "L0_gnn_fc1_w1", "L0_gnn_fc1_b1", "L0_gnn_bn0_gs", "L0_gnn_bn0_bs", "L0_gnn_bn0_gv",
            "L0_gnn_bn1_gs", "L0_gnn_bn1_bs", "L1_gnn_W1", "L1_gnn_b1", "L1_gnn_W2", "L1_gnn_b2", "L1_gnn_W3", "L1_gnn_b3"]


def lay_out(inputs):
    import numpy as np

    arrays = {name: np.ascontiguousarray(inputs[name]) for name in ["x", *_WEIGHTS]}
    for name in ("src", "dst"):
        cols = np.asarray(inputs[name]).reshape(NG, P, T)
        arrays[f"{name}_cols"] = np.ascontiguousarray(cols)
        arrays[f"{name}_rows"] = np.ascontiguousarray(cols.transpose(0, 2, 1))
    arrays["ev_cols"] = np.ascontiguousarray(np.asarray(inputs["edge_attr_3"]).reshape(NG, P, T * NC))
    arrays["ea_t"] = np.ascontiguousarray(np.asarray(inputs["edge_attr_48"]).reshape(NG, P, T, FE).transpose(0, 3, 2, 1)).reshape(NG, FE, GE)
    for i in range(2):
        w = np.concatenate([np.asarray(inputs[f"L0_gnn_fc{i}_w2"]), np.asarray(inputs[f"L0_gnn_fc{i}_b2"])[None]])
        if i == 0:
            scalars = w[:, :NS * NS].reshape(FE + 1, NS, NS).transpose(0, 2, 1)
            vectors = w[:, NS * NS:].reshape(FE + 1, NS, NV).transpose(0, 2, 1)
            w = np.concatenate([vectors, scalars], axis=1)
        else:
            w = w.reshape(FE + 1, NS + NV, NS).transpose(0, 2, 1)
        arrays[f"w2_{i}"] = np.ascontiguousarray(w.reshape(FE + 1, WN))
    e, b = np.arange(P)[:, None], np.arange(NB)[None, :]
    arrays["powers"] = np.where(e // BITS == b, 2.0 ** (BITS - 1 - e % BITS), 0.0).astype(np.float32)
    arrays["before"] = np.where(e // BITS == b, 1.0, np.where(e // BITS > b, 2.0 ** BITS, 0.0)).astype(np.float32)
    arrays["limit"] = (2.0 ** (BITS - e % BITS)).astype(np.float32)
    return arrays


def kernel(**inputs):
    import concourse.bacc as bacc
    from concourse.bass_utils import run_bass_kernel_spmd

    nc = bacc.Bacc("TRN2", target_bir_lowering=False, num_devices=1)
    arrays = lay_out(inputs)
    a = {name: nc.dram_tensor(f"in_{name}", v.shape, mybir.dt.from_np(v.dtype), kind="ExternalInput").ap() for name, v in arrays.items()}
    out = nc.dram_tensor("out_nodes", (N, NS), F32, kind="ExternalOutput").ap()
    build(nc, a, out)
    r = run_bass_kernel_spmd(nc, [{f"in_{name}": v for name, v in arrays.items()}], core_ids=[0])
    return r.results[0]["out_nodes"]
```
